# Optimizing a Trainium2 kernel written in Bass

```python
import numpy as np
import jax
import jax.numpy as jnp

def _softmax(x, axis=-1):
    return jax.nn.softmax(x, axis=axis)

def _gelu(x):
    return jax.nn.gelu(x, approximate=True)

def _silu(x):
    return jax.nn.silu(x)

def _sigmoid(x):
    return jax.nn.sigmoid(x)

def _layernorm(x, axis=-1, eps=1e-05):
    m = jnp.mean(x, axis=axis, keepdims=True)
    v = jnp.var(x, axis=axis, keepdims=True)
    return (x - m) / jnp.sqrt(v + eps)

def _scatter_add(tgt, idx, src, axis=0):
    return tgt.at[idx].add(src)

def _segment_sum(src, seg, n):
    return jax.ops.segment_sum(src, seg, n)
kernel_name = 'mk_macaron_d1_jaxref_r8_beb9ea'

def setup_inputs(seed: int=0):
    np.random.seed(seed)
    _w = jnp.asarray

    def _L0_attn_setup():
        import jax, jax.numpy as jnp
        import numpy as np
        D_MODEL = 128
        N_HEAD = 16
        HEAD_DIM = D_MODEL // N_HEAD
        EPS = 1e-06
        B, T = (4, 128)

        def _eml(x, agg, eps=EPS):
            return jnp.log(jnp.abs(x) + eps) - jnp.log(agg + eps)

        def _split_heads(t):
            b, s, _ = t.shape
            return t.reshape(b, s, N_HEAD, HEAD_DIM).transpose(0, 2, 1, 3)
        key = jax.random.key(seed)
        k0, k1, k2, k3 = jax.random.split(key, 4)
        x = jax.random.normal(k0, (B, T, D_MODEL), dtype=jnp.float32)
        bound = 0.1 / np.sqrt(D_MODEL)
        w_qkv = jax.random.uniform(k1, (3 * D_MODEL, D_MODEL), jnp.float32, -bound, bound)
        w_ky = jax.random.uniform(k2, (D_MODEL, D_MODEL), jnp.float32, -bound, bound)
        w_proj = jax.random.uniform(k3, (D_MODEL, D_MODEL), jnp.float32, -bound, bound)
        return {'x': x, 'w_qkv': w_qkv, 'w_ky': w_ky, 'w_proj': w_proj}
    _L0_attn_in = _L0_attn_setup()

    def _L0_ffn_setup():
        import jax, jax.numpy as jnp
        import numpy as np
        S, N, D, F, E = (256, 8, 128, 512, 8)
        STD = 0.02
        key = jax.random.key(seed)
        ks = jax.random.split(key, 5)
        x = jax.random.normal(ks[0], (S, N, D), dtype=jnp.float32)
        Wg = jax.random.normal(ks[1], (E, D), dtype=jnp.float32) * STD
        W1 = jax.random.normal(ks[2], (E, F, D), dtype=jnp.float32) * STD
        b1 = jnp.zeros((E, F), dtype=jnp.float32)
        W2 = jax.random.normal(ks[3], (E, D, F), dtype=jnp.float32) * STD
        b2 = jnp.zeros((E, D), dtype=jnp.float32)
        return {'x': x, 'Wg': Wg, 'W1': W1, 'b1': b1, 'W2': W2, 'b2': b2}
    _L0_ffn_in = _L0_ffn_setup()
    _d = {'L0_attn_x': _L0_attn_in['x'], 'L0_attn_w_qkv': _L0_attn_in['w_qkv'], 'L0_attn_w_ky': _L0_attn_in['w_ky'], 'L0_attn_w_proj': _L0_attn_in['w_proj'], 'L0_ffn_Wg': _L0_ffn_in['Wg'], 'L0_ffn_W1': _L0_ffn_in['W1'], 'L0_ffn_b1': _L0_ffn_in['b1'], 'L0_ffn_W2': _L0_ffn_in['W2'], 'L0_ffn_b2': _L0_ffn_in['b2']}
    _x0 = _d['L0_attn_x']
    _d['L0_attn_x'] = jax.random.normal(jax.random.fold_in(jax.random.key(seed), 1), (4, 512, 128), dtype=_x0.dtype)
    del _x0
    return _d

def reference(L0_attn_x, L0_attn_w_qkv, L0_attn_w_ky, L0_attn_w_proj, L0_ffn_Wg, L0_ffn_W1, L0_ffn_b1, L0_ffn_W2, L0_ffn_b2):

    def _L0_attn_ref(x, w_qkv, w_ky, w_proj):
        import jax, jax.numpy as jnp
        import numpy as np
        D_MODEL = 128
        N_HEAD = 16
        HEAD_DIM = D_MODEL // N_HEAD
        EPS = 1e-06
        B, T = (4, 128)

        def _eml(x, agg, eps=EPS):
            return jnp.log(jnp.abs(x) + eps) - jnp.log(agg + eps)

        def _split_heads(t):
            b, s, _ = t.shape
            return t.reshape(b, s, N_HEAD, HEAD_DIM).transpose(0, 2, 1, 3)
        b, t, _ = x.shape
        qkv = x @ w_qkv.T
        q, k, v = jnp.split(qkv, 3, axis=-1)
        q, k, v = (_split_heads(q), _split_heads(k), _split_heads(v))
        scale = 1.0 / np.sqrt(HEAD_DIM)
        L = jnp.einsum('bhqd,bhkd->bhqk', q, k) * scale
        mask = jnp.tril(jnp.ones((t, t), dtype=L.dtype))[None, None]
        k_y = _split_heads(x @ w_ky.T)
        L_y = jnp.einsum('bhqd,bhkd->bhqk', q, k_y) * scale
        agg = jnp.sum(jnp.exp(jnp.clip(L_y, -15.0, 15.0)) * mask, axis=-1, keepdims=True) + EPS
        r = _eml(L, agg)
        w = jax.nn.softplus(r) * mask
        A = w / (jnp.sum(w, axis=-1, keepdims=True) + EPS)
        out = jnp.einsum('bhqk,bhkd->bhqd', A, v)
        out = out.transpose(0, 2, 1, 3).reshape(b, t, D_MODEL)
        return out @ w_proj.T

    def _L0_ffn_ref(x, Wg, W1, b1, W2, b2):
        import jax, jax.numpy as jnp
        import numpy as np
        S, N, D, F, E = (256, 8, 128, 512, 8)
        STD = 0.02
        scores = jnp.einsum('snd,ed->sne', x, Wg)
        prob = jax.nn.softmax(scores, axis=-1)
        top1_idx = jnp.argmax(prob, axis=-1)
        top1_prob = jnp.take_along_axis(prob, top1_idx[..., None], axis=-1)[..., 0]
        y = jnp.zeros_like(x)
        n_experts = Wg.shape[0]
        for e in range(n_experts):
            h = jax.nn.gelu(jnp.einsum('snd,fd->snf', x, W1[e]) + b1[e], approximate=False)
            ye = jnp.einsum('snf,df->snd', h, W2[e]) + b2[e]
            mask = (top1_idx == e)[..., None]
            y = y + jnp.where(mask, ye * top1_prob[..., None], 0.0)
        return y
    x = L0_attn_x
    x = x + 0.5 * _L0_ffn_ref(_layernorm(x, axis=-1), L0_ffn_Wg, L0_ffn_W1, L0_ffn_b1, L0_ffn_W2, L0_ffn_b2)
    x = x + _L0_attn_ref(_layernorm(x, axis=-1), L0_attn_w_qkv, L0_attn_w_ky, L0_attn_w_proj)
    x = x + 0.5 * _L0_ffn_ref(_layernorm(x, axis=-1), L0_ffn_Wg, L0_ffn_W1, L0_ffn_b1, L0_ffn_W2, L0_ffn_b2)
    return x

_drawn_inputs = setup_inputs


def setup_inputs(seed=0):
    import zlib

    import numpy as np

    out = dict(_drawn_inputs(seed))
    spreads = {'L0_ffn_b1': (0.0, 0.8), 'L0_ffn_b2': (0.0, 0.457)}
    factors = {'L0_attn_w_qkv': 8.0,
     'L0_attn_w_ky': 8.0,
     'L0_attn_w_proj': 8.0,
     'L0_ffn_Wg': 2.965,
     'L0_ffn_W1': 5.925,
     'L0_ffn_W2': 5.367}
    for name, (base, spread) in spreads.items():
        noise = np.random.default_rng([zlib.crc32(name.encode()), seed]).standard_normal(out[name].shape)
        drawn = base * np.exp(spread * noise) if base else spread * noise
        out[name] = jnp.asarray(drawn.astype(out[name].dtype))
    for name, factor in factors.items():
        out[name] = (out[name] * factor).astype(out[name].dtype)
    return out
```

```python
import numpy as np
import concourse.bass as bass
from concourse import mybir
from contextlib import ExitStack, contextmanager

P = 128
NT = 16
NB, TB = 4, 4
SEQ = TB * P
E, F = 8, 512
FC = F // P
NS = NT + E - 1
H, HD = 16, 8
HP = H // 2
TERMS = 3
Q_TERMS = (0, 0, 1, 1, 0, 2)
K_TERMS = (0, 1, 0, 1, 2, 0)
KROWS = HD * len(Q_TERMS)
EXP_AND_LN = 6
EPS = 1e-6
LN_EPS = 1e-5
SCALE = float(1.0 / np.sqrt(HD))
CLIP = 15.0 / SCALE
MASKED = -3.0e4
STEPS = NB * HP
LAG = HP + 4
SEG_J = ((0,), (3, 1), (2,))
SEG_N = (512, 512, 256)
SEG_MASK = (128, 0, 128)
QUAD = 32
J_OFF = {0: 0, 3: 512, 1: 640, 2: 1024}
HEAD_W = 1280
STACK_DMAS = 16 * 2 * len(Q_TERMS)
GROUPS = -(-NS // 4)
R_AT = HP - 1
Q_AT = R_AT + 2
C_AT = LAG + HP - 1
N_AT = LAG + HP + 1
T_AT = N_AT + 1
O_AT = T_AT + 1
P_AT = O_AT + 1
X_AT = P_AT + 1
LAST_STEP = STEPS + LAG + 2
END_STEP = (NB - 1) * HP + X_AT + 1


def stretches(breaks):
    cuts = {0, 2, LAG, LAG + 2, LAG + 4, STEPS, STEPS + LAG, LAST_STEP, END_STEP} | {s + 1 for s in breaks}
    cuts = sorted(c for c in cuts if c <= END_STEP)
    return list(zip(cuts[:-1], cuts[1:]))


@contextmanager
def steps(engine, s0, s1):
    if s1 - s0 == 2 or s0 >= LAST_STEP:
        yield s0
    else:
        with engine.Fori(s0 // 2, s1 // 2) as m:
            yield m * 2


def build(nc, x_in, wattn_in, wg_in, w1_in, b1_in, w2_in, b2_in, out):
    f32, bf16, u32, i32 = mybir.dt.float32, mybir.dt.bfloat16, mybir.dt.uint32, mybir.dt.int32
    ALU, ACT, AX = mybir.AluOpType, mybir.ActivationFunctionType, mybir.AxisListType.X
    ds = bass.ds
    ctx = ExitStack()
    with ctx:
        def sb(name, shape, dt=f32):
            return ctx.enter_context(nc.sbuf_tensor(name, shape, dt))

        def sem(name):
            return ctx.enter_context(nc.semaphore(name))

        X = sb("X", [P, NT, P])
        R1 = sb("R1", [P, 8192])
        W1 = R1[:, 0:4096]
        W2 = R1[:, 4096:8192]
        XN2 = R1[:, 0:2048].rearrange("p (n d) -> p n d", n=NT)
        XNT2 = R1[:, 2048:4096]
        REM = R1[:, 4096:5120].rearrange("p (r n) -> p r n", r=2)
        WB = R1[:, 0:5120].rearrange("p (r n) -> p r n", r=2)
        QP3 = R1[:, 5120:5888].bitcast(bf16).rearrange("p (t n) -> p t n", t=TERMS)
        AOT = R1[:, 5888:6400]
        AO = R1[:, 6400:6976].rearrange("p (i h c) -> p i h c", i=TB, h=H)
        NUM = R1[:, 6976:7488].rearrange("p (i h c) -> p i h c", i=TB, h=H)
        OT = R1[:, 7488:8000]
        QREM = OT
        R2 = sb("R2", [P, 4608])
        XN1 = R2[:, 0:2048].rearrange("p (n d) -> p n d", n=NT)
        XNT1 = R2[:, 2048:4096]
        R2B = R2[:, :].bitcast(bf16).rearrange("p (r t n) -> p r t n", r=3, t=TERMS)
        R3 = sb("R3", [P, 24576])
        stacks = R3[:, :].bitcast(bf16).rearrange("p (s q n) -> p s q n", s=3, q=HP)
        QS, YS, KS = stacks[:, 0], stacks[:, 1], stacks[:, 2]
        XS = R3[:, 0:NS * P].rearrange("p (s d) -> p s d", s=NS)
        YO = R3[:, 2944:2944 + NS * P].rearrange("p (s d) -> p s d", s=NS)
        YG = R3[:, 5888:7936].rearrange("p (n d) -> p n d", n=NT)
        HB = R3[:, 7936:8960].rearrange("p (r n) -> p r n", r=2)
        HT = R3[:, 8960:9984].rearrange("p (r n) -> p r n", r=2)
        BS = R3[0:TERMS, 9984:12544].bitcast(bf16)
        BL = R3[0:E, 12544:13184]
        BR = R3[0:E, 13184:13824]
        BT = R3[0:E, 13824:14784].bitcast(bf16).rearrange("p (t n) -> p t n", t=TERMS)
        XT = R3[:, 14784:15808].rearrange("p (r n) -> p r n", r=2)
        T3 = R3[:, 16384:24576]
        sh = T3[:, 0:128].rearrange("p (n e) -> p n e", n=NT)
        ex = T3[:, 128:256].rearrange("p (n e) -> p n e", n=NT)
        cand = T3[:, 256:384].rearrange("p (n e) -> p n e", n=NT)
        posm = T3[:, 384:512].rearrange("p (n e) -> p n e", n=NT)
        ntc = T3[:, 512:640].rearrange("p (e j) -> p e j", e=E)
        bsm = T3[:, 640:704].rearrange("p (e j) -> p e j", e=E)
        mapm = T3[:, 704:704 + NS * E].rearrange("p (s e) -> p s e", s=NS)
        rt = sb("rt", [P, 5, TB * H])
        mx, cmin, ssum, posf = (T3[:, 896 + 16 * k:912 + 16 * k] for k in range(4))
        cnt, nt, bst, brow, bend = (T3[:, 960 + 8 * k:968 + 8 * k] for k in range(5))
        mapf = T3[:, 1000:1000 + NS]
        oh = T3[:, 1024:1092].bitcast(bf16).rearrange("p (n e) -> p n e", n=NT + 1)
        stats = T3[:, 1100:1196].rearrange("p (n s) -> p n s", n=NT)
        mv = T3[:, 1200:1232].rearrange("p (n s) -> p n s", n=NT)
        lnt = T3[:, 1232:1296].rearrange("p (k n) -> p k n", k=4)
        QT = sb("QT", [P, NT, P])
        VF = sb("V", [P, NT * H * (HD + 1) + QUAD])
        V = VF[:, 0:NT * H * (HD + 1)].rearrange("p (n h c) -> p n h c", n=NT, h=H)
        QPS = sb("QPS", [P, 2, HP, SEQ], bf16)
        QB = QPS[:, :, :, :].rearrange("p r q n -> p (r q n)")[:, 0:2 * TERMS * 2 * SEQ]\
            .rearrange("p (r t n) -> p r t n", r=2, t=TERMS)
        SP3 = (R2B[:, 0], R2B[:, 1], R2B[:, 2], QB[:, 0], QB[:, 1], R2B[:, 0])
        CL = sb("CL", [P, 2, 2, SEQ])
        WA = sb("WA", [P, 5, P])
        WG = sb("WG", [P, E])
        ident = sb("ident", [P, P])
        tri = sb("tri", [P, P])
        ones = sb("ones", [P, P])
        MA = sb("MA", [P, SEQ])
        MB = sb("MB", [P, 5 * P], i32)
        utri = sb("utri", [P, P], bf16)
        onesb = sb("onesb", [P, P], bf16)
        em8 = sb("em8", [P, E])
        j128 = sb("j128", [P, NT])
        lower8 = sb("lower8", [P, E, E])
        slot_no = sb("slot_no", [P, NS])
        seen = sb("seen", [P, TB])
        agg = sb("agg", [P, TB, 2, STEPS])
        ck = sb("ck", [P, 2, TB, H])
        coef = sb("coef", [P, NT])
        posi = sb("posi", [P, NT], u32)
        emap = sb("emap", [P, NS], u32)
        PS = ctx.enter_context(nc.psum_tensor("PS", [P, 8, 512], f32))
        xs_d = [nc.dram_tensor(f"xs{r}_d", (NS * P, P), f32, kind="Internal").ap() for r in range(2)]
        ys_d = [nc.dram_tensor(f"ys{r}_d", (NS * P, P), f32, kind="Internal").ap() for r in range(2)]
        bs_d = nc.dram_tensor("bias_terms_d", (TERMS, E * (F + P)), bf16, kind="Internal").ap()

        s_x = sem("x_loaded")
        s_wa = sem("attn_weights_loaded")
        s_w = sem("expert_weights_loaded")
        s_b = sem("biases_loaded")
        s_bt = sem("bias_terms_ready")
        s_bd = sem("bias_terms_stored")
        s_bs = sem("bias_rows_loaded")
        s_z = sem("zero_tile_ready")
        s_zd = sem("scratch_zeroed")
        s_c0 = sem("const_fill")
        s_c = sem("consts_ready")
        s_dve = sem("dve_chain")
        s_var = sem("variance_ready")
        s_std = sem("std_ready")
        s_xn = sem("xn_ready")
        s_tp = sem("xnt_transposed")
        s_xnt = sem("xnt_copied")
        s_sc = sem("scores_ready")
        s_sh = sem("shifted_scores")
        s_ex = sem("exp_scores")
        s_oh = sem("onehot_ready")
        s_rk = sem("ranks_ready")
        s_pos = sem("positions_ready")
        s_sct = sem("rows_scattered")
        s_xs = [[sem(f"slots_{r}_{g}_loaded") for g in range(GROUPS)] for r in range(2)]
        s_px = sem("slot_transposed")
        s_vx = sem("slot_t_copied")
        s_up = sem("up_done")
        s_h = sem("gelu_done")
        s_ph = sem("hidden_transposed")
        s_vh = sem("hidden_t_copied")
        s_dn = sem("down_done")
        s_y = sem("y_copied")
        s_yd = sem("y_stored")
        s_yg = [sem(f"y_{b}_gathered") for b in range(NB)]
        s_xr = sem("residual_ready")
        s_pj = sem("projection_done")
        s_hi = sem("first_term_ready")
        s_rem = sem("remainder_ready")
        s_lo = sem("terms_ready")
        s_mid = sem("second_term_ready")
        s_stk = [sem(f"stack_{i}_written") for i in range(6)]
        s_qv = sem("qv_done")
        s_qc = sem("q_copied")
        s_vc = sem("v_copied")
        s_pa = sem("ly_ready")
        s_cl = sem("clipped")
        s_e = sem("exp_summed")
        s_qsc = sem("q_scaled")
        s_qt = sem("scaled_q_transposed")
        s_qhi = sem("scaled_q_first_term")
        s_qrem = sem("scaled_q_remainder")
        s_qmid = sem("scaled_q_second_term")
        s_qlo = sem("scaled_q_terms_ready")
        s_qps = sem("scaled_q_stacked")
        s_pb = sem("l_ready")
        s_abs = sem("abs_done")
        s_ln = sem("ln_done")
        s_av = sem("av_done")
        s_aot = sem("av_out_of_psum")
        s_aotp = sem("av_transposed")
        s_ao = sem("av_copied")
        s_cv = sem("v_prefix_done")
        s_num = sem("attn_out_ready")
        s_ot = sem("attn_out_transposed")
        s_otc = sem("attn_out_t_copied")
        s_pr = sem("attn_projected")
        s_out = sem("output_stored")

        aggf = agg[:, :, :, :].rearrange("p i par s -> p (i par s)")
        UNITS = ((0, 0), (1, 0), (2, 0), (0, 1), (1, 1), (2, 1))
        WCOL = (0, 2, 3)

        def stack_rows(par, t):
            return slice(64 * par + HD * t, 64 * par + HD * t + HD)

        def half(w):
            return slice(w * 2 * SEQ, (w + 1) * 2 * SEQ)

        def spread(a, axis, n):
            shape = list(a.shape)
            shape[axis] = n
            return a.broadcast_to(shape)

        def ckf(b):
            return ck[:, b % 2, :, :].rearrange("p i h -> p (i h)")

        block = ctx.enter_context(nc.Block())


        @block.sync
        def _(sp):
            sp.dma_start(X[:, :, :], x_in.rearrange("(n p) d -> p n d", p=P)).then_inc(s_x, 16)
            sp.dma_start(WG[:, :], wg_in).then_inc(s_x, 16)
            sp.dma_start(BL[:, 0:F], b1_in).then_inc(s_b, 16)
            sp.dma_start(BL[:, F:F + P], b2_in).then_inc(s_b, 16)
            sp.wait_ge(s_z, 1)
            for r in range(2):
                sp.dma_start(xs_d[r].rearrange("(s p) d -> p s d", p=P), XS).then_inc(s_zd, 16)
            sp.wait_ge(s_bt, 1)
            sp.dma_start(bs_d.rearrange("t (e n) -> e t n", e=E), BT).then_inc(s_bd, 16)
            sp.wait_ge(s_bd, 16)
            sp.dma_start(BS, bs_d).then_inc(s_bs, 16)
            sp.dma_start(WA[:, :, :], wattn_in).then_inc(s_wa, 16)

            def slots(r):
                sp.wait_ge(s_sct, 16 * NT * (r + 1))
                for g in range(0, NS, 4):
                    s1 = min(g + 4, NS)
                    sp.dma_start(XS[:, g:s1, :],
                                 xs_d[r][g * P:s1 * P, :].rearrange("(s p) d -> p s d", p=P))\
                        .then_inc(s_xs[r][g // 4], 16)
                with sp.Fori(0, NS) as s:
                    sp.wait_ge(s_y, s + (r * NS + 1))
                    sp.dma_start(ys_d[r][ds(s * P, P), :], YO[:, ds(s, 1), :]).then_inc(s_yd, 16)

            slots(0)
            for u, (which, w) in enumerate(UNITS):
                sp.wait_ge(s_lo, 2 * (u + 1))
                dst = (QS, YS, KS)[which]
                for t, term in enumerate(K_TERMS if which else Q_TERMS):
                    for par in range(2):
                        sp.dma_start(dst[stack_rows(par, t), :, half(w)],
                                     SP3[u][64 * par:64 * par + 64, term, :]).then_inc(s_stk[u], 16)
            sp.wait_ge(s_stk[3], STACK_DMAS)
            sp.wait_ge(s_stk[4], STACK_DMAS)
            for b in range(NB):
                sp.wait_ge(s_qlo, b + 1)
                if b >= 2:
                    sp.wait_ge(s_pb, 6 * HP * (b - 1))
                for t, term in enumerate(Q_TERMS):
                    for par in range(2):
                        sp.dma_start(QPS[stack_rows(par, t), b % 2, :, :],
                                     QP3[64 * par:64 * par + 64, term, :]).then_inc(s_qps, 16)
            sp.wait_ge(s_pb, 6 * STEPS)
            sp.dma_start(BS, bs_d).then_inc(s_bs, 16)
            sp.wait_ge(s_av, STEPS)
            sp.dma_start(W1, w1_in).then_inc(s_w, 16)
            sp.wait_ge(s_pr, NB)
            sp.dma_start(W2, w2_in).then_inc(s_w, 16)
            slots(1)
            for b in range(NB):
                sp.wait_ge(s_xr, NT + NB + TB * (b + 1))
                sp.dma_start(out[b * SEQ:(b + 1) * SEQ, :].rearrange("(n p) d -> p n d", p=P),
                             X[:, b * TB:(b + 1) * TB, :]).then_inc(s_out, 16)
            sp.wait_ge(s_out, 16 * NB)

        @block.gpsimd
        def _(pool):
            pool.memset(XS, 0.0).then_inc(s_z, 1)
            pool.memset(ident[:, :], 0.0).then_inc(s_c0, 1)
            pool.memset(tri[:, :], 1.0).then_inc(s_c0, 1)
            pool.memset(ones[:, :], 1.0).then_inc(s_c0, 1)
            pool.memset(utri[:, :], 1.0).then_inc(s_c0, 1)
            pool.memset(onesb[:, :], 1.0).then_inc(s_c0, 1)
            pool.memset(MA[:, :], CLIP).then_inc(s_c0, 1)
            pool.memset(MB[:, :], -1).then_inc(s_c0, 1)
            pool.memset(VF[:, :], 1.0).then_inc(s_c0, 1)
            ok = dict(allow_small_or_imprecise_dtypes=True)
            pool.iota(em8[:, :], [[1, E]], base=-E, channel_multiplier=0, **ok).then_inc(s_c0, 1)
            pool.iota(j128[:, :], [[P, NT]], base=0, channel_multiplier=0, **ok).then_inc(s_c0, 1)
            pool.iota(lower8[:, :, :], [[1, E], [-1, E]], base=0, channel_multiplier=0, **ok)\
                .then_inc(s_c0, 1)
            pool.iota(slot_no[:, :], [[1, NS]], base=0, channel_multiplier=0, **ok).then_inc(s_c0, 1)
            pool.iota(seen[:, :], [[P, TB]], base=1, channel_multiplier=1, **ok).then_inc(s_c0, 1)
            pool.wait_ge(s_c0, 13)
            pool.affine_select(out=ident[:, :], in_=ident[:, :], compare_op=ALU.not_equal, fill=1.0,
                               base=0, pattern=[[-1, P]], channel_multiplier=1).then_inc(s_c, 1)
            pool.affine_select(out=tri[:, :], in_=tri[:, :], compare_op=ALU.is_ge, fill=0.0,
                               base=0, pattern=[[1, P]], channel_multiplier=-1).then_inc(s_c, 1)
            pool.affine_select(out=utri[:, :], in_=utri[:, :], compare_op=ALU.is_gt, fill=0.0,
                               base=0, pattern=[[1, P]], channel_multiplier=-1).then_inc(s_c, 1)
            pool.affine_select(out=MA[:, SEQ - P:SEQ], in_=MA[:, SEQ - P:SEQ], compare_op=ALU.is_ge,
                               fill=MASKED, base=0, pattern=[[-1, P]], channel_multiplier=1)\
                .then_inc(s_c, 1)
            for at in (0, P):
                pool.affine_select(out=MB[:, at:at + P], in_=MB[:, at:at + P], compare_op=ALU.is_ge,
                                   fill=0, base=0, pattern=[[1, P]], channel_multiplier=-1)\
                    .then_inc(s_c, 1)
            pool.tensor_scalar(lower8[:, :, :], lower8[:, :, :], 0.0, None, ALU.is_gt).then_inc(s_c, 1)

            def scatter(r):
                pool.wait_ge(s_pos, 2 * r + 1)
                if r == 0:
                    pool.wait_ge(s_zd, 32)
                for n in range(NT):
                    pool.indirect_dma_start(xs_d[r], bass.IndirectOffsetOnAxis(posi[:, n:n + 1], 0),
                                            XN1[:, n, :], None).then_inc(s_sct, 16)

            def gather(r):
                pool.wait_ge(s_yd, 16 * NS * (r + 1))
                for n in range(NT):
                    pool.indirect_dma_start(YG[:, n, :], None, ys_d[r],
                                            bass.IndirectOffsetOnAxis(posi[:, n:n + 1], 0))\
                        .then_inc(s_yg[n // TB], 16)

            scatter(0)
            gather(0)
            for u in range(len(UNITS)):
                for c in range(2):
                    m = 2 * u + c
                    pool.wait_ge(s_rem, m + 1)
                    pool.tensor_copy(SP3[u][:, 1, c * SEQ:(c + 1) * SEQ], REM[:, c, :])\
                        .then_inc(s_mid, 1)
                    pool.wait_ge(s_mid, m + 1)
                    pool.tensor_tensor(SP3[u][:, 2, c * SEQ:(c + 1) * SEQ], REM[:, c, :],
                                       SP3[u][:, 1, c * SEQ:(c + 1) * SEQ], ALU.subtract)\
                        .then_inc(s_lo, 1)
            for b in range(NB):
                pool.wait_ge(s_qrem, b + 1)
                if b:
                    pool.wait_ge(s_qps, 16 * 2 * len(Q_TERMS) * b)
                pool.tensor_copy(QP3[:, 1, :], QREM).then_inc(s_qmid, 1)
                pool.wait_ge(s_qmid, b + 1)
                pool.tensor_tensor(QP3[:, 2, :], QREM, QP3[:, 1, :], ALU.subtract).then_inc(s_qlo, 1)
            scatter(1)
            gather(1)

        @block.scalar
        def _(act):
            def tables(number):
                act.add_instruction(mybir.InstLoadActFuncSet(
                    name=nc.get_next_instruction_name(), act_func_set_id=number,
                    engine=mybir.EngineType.Activation, ins=[], outs=[]))

            act.dma_start(W1, w1_in).then_inc(s_w, 16)
            act.dma_start(W2, w2_in).then_inc(s_w, 16)

            def layer_norm(k, xnt):
                act.wait_ge(s_var, k + 1)
                act.activation(lnt[:, 1, :], lnt[:, 0, :], ACT.Sqrt).then_inc(s_std, 1)
                for g in range(NB):
                    act.wait_ge(s_tp, NB * k + g + 1)
                    act.activation(xnt[:, g * SEQ:(g + 1) * SEQ], PS[:, g % 2, :], ACT.Copy)\
                        .then_inc(s_xnt, 1)

            def gelu(r, s, par, first):
                act.wait_ge(s_up, s + (r * NS + 1))
                if not first:
                    act.wait_ge(s_ph, s + (r * NS - 1))
                act.activation(HB[:, par, :], PS[:, par, :], ACT.Gelu).then_inc(s_h, 1)

            def copy_xt(r, g, w):
                act.wait_ge(s_px, g + (r * GROUPS + 1))
                act.activation(XT[:, ds(g & 1, 1), 0:w], PS[:, ds((g & 1) + 4, 1), 0:w],
                               ACT.Copy).then_inc(s_vx, 1)

            def ffn(r):
                layer_norm(2 * r, XNT1)
                act.wait_ge(s_sh, r + 1)
                act.activation(ex, sh, ACT.Exp).then_inc(s_ex, 1)
                copy_xt(r, 0, SEQ)

                def group(g, width, first):
                    for k in range(width):
                        gelu(r, 4 * g + k, k % 2, first and k < 2)
                        if k == 1:
                            copy_xt(r, g + 1, SEQ)

                group(0, 4, r == 0)
                with act.Fori(1, GROUPS - 2) as g:
                    group(g, 4, False)
                for k in range(4):
                    gelu(r, 4 * (GROUPS - 2) + k, k % 2, False)
                    if k == 1:
                        copy_xt(r, GROUPS - 1, (NS - 4 * (GROUPS - 1)) * P)
                for s in range(4 * (GROUPS - 1), NS):
                    gelu(r, s, s % 2, False)

            ffn(0)
            layer_norm(1, XNT2)

            def first_term(m):
                u, c = m // 2, m % 2
                act.wait_ge(s_pj, m + 1)
                if u == 5:
                    act.wait_ge(s_stk[0], STACK_DMAS)
                act.activation(SP3[u][:, 0, c * SEQ:(c + 1) * SEQ], PS[:, c, :], ACT.Copy)\
                    .then_inc(s_hi, 1)

            def q_rows(t):
                act.wait_ge(s_qv, t + 1)
                act.activation(QT[:, 2 * t:2 * t + 2, :],
                               PS[:, 2 + t % 2, :].rearrange("p (n c) -> p n c", n=2)[:, :, 0:P],
                               ACT.Copy).then_inc(s_qc, 1)

            for m in range(6):
                first_term(m)
            for t in range(NT // 2):
                q_rows(t)
            for m in range(6, 12):
                first_term(m)

            def first_pass(s, tiles):
                for i in tiles:
                    n = (i + 1) * P
                    act.wait_ge(s_cl, 4 * s + (i + 1))
                    for par in range(2):
                        act.activation(CL[:, i % 2, par, 0:n], CL[:, i % 2, par, 0:n], ACT.Exp,
                                       scale=SCALE,
                                       accum_out=aggf[:, ds(s + (2 * i + par) * STEPS, 1)])\
                            .then_inc(s_e, 1)

            def second_pass(v):
                act.wait_ge(s_abs, 6 * v + 6)
                act.activation(WB[:, ds(v & 1, 1), :], WB[:, ds(v & 1, 1), :], ACT.Ln,
                               bias=1.0, scale=1.0).then_inc(s_ln, 1)

            def av_out(v):
                act.wait_ge(s_av, v + 1)
                act.activation(AOT, PS[:, 6, :], ACT.Copy).then_inc(s_aot, 1)

            breaks = [b * HP + k for b in range(NB) for k in (Q_AT, O_AT)]
            tables(EXP_AND_LN)
            for s0, s1 in stretches(breaks):
                with steps(act, s0, s1) as base:
                    for odd in range(2):
                        s = base + odd
                        if s0 < STEPS:
                            first_pass(s, (0, 1))
                        if odd and LAG + 2 <= s0 < LAST_STEP:
                            av_out(s - LAG - 2)
                        if s0 < STEPS:
                            first_pass(s, (2, 3))
                        if LAG <= s0 < STEPS + LAG:
                            second_pass(s - LAG)
                for b in range(NB):
                    if s1 == b * HP + Q_AT + 1:
                        act.wait_ge(s_qt, b + 1)
                        if b:
                            act.wait_ge(s_qps, STACK_DMAS * b)
                        act.activation(QP3[:, 0, :], PS[:, 7, :], ACT.Copy).then_inc(s_qhi, 1)
                    if s1 == b * HP + O_AT + 1:
                        act.wait_ge(s_ot, b + 1)
                        act.wait_ge(s_qlo, min(b + 2, NB))
                        act.activation(OT, PS[:, 7, :], ACT.Copy).then_inc(s_otc, 1)
            ffn(1)

        @block.vector
        def _(dve):
            done = [0]

            def mark(ins, times=1):
                done[0] += times
                ins.then_inc(s_dve, 1)

            def settle():
                dve.wait_ge(s_dve, done[0])

            def link(ins):
                mark(ins)
                settle()

            def layer_norm(k, xn):
                for n in range(NT):
                    mark(dve.bn_stats(stats[:, n, :], X[:, n, :]))
                settle()
                for n in range(NT):
                    mark(dve.bn_aggr(mv[:, n, :], stats[:, n, :]))
                settle()
                dve.tensor_scalar(lnt[:, 0, :], mv[:, :, 1], LN_EPS, None, ALU.add).then_inc(s_var, 1)
                dve.wait_ge(s_std, k + 1)
                link(dve.reciprocal(lnt[:, 2, :], lnt[:, 1, :]))
                link(dve.tensor_tensor(lnt[:, 3, :], lnt[:, 2, :], lnt[:, 2, :], ALU.mult))
                link(dve.tensor_tensor(lnt[:, 3, :], lnt[:, 3, :], lnt[:, 0, :], ALU.mult))
                link(dve.tensor_scalar(lnt[:, 3, :], lnt[:, 3, :], -0.5, 1.5, ALU.mult, ALU.add))
                link(dve.tensor_tensor(lnt[:, 2, :], lnt[:, 2, :], lnt[:, 3, :], ALU.mult))
                for n in range(NT):
                    dve.tensor_scalar(xn[:, n, :], X[:, n, :], mv[:, n, 0:1], lnt[:, 2, n:n + 1],
                                      ALU.subtract, ALU.mult).then_inc(s_xn, 1)

            def over_n(a, k=NT):
                return spread(a.rearrange("p (o e) -> p o e", o=1), 1, k)

            def over_e(a, k=E):
                return spread(a.rearrange("p (n o) -> p n o", o=1), 2, k)

            def route(r):
                dve.wait_ge(s_sc, r + 1)
                sc = PS[:, 2, 0:NT * E].rearrange("p (n e) -> p n e", n=NT)
                link(dve.memset(oh[:, NT, :], 0.0))
                link(dve.reduce_max(mx, sc, axis=AX))
                dve.tensor_tensor(sh, sc, over_e(mx), ALU.subtract).then_inc(s_sh, 1)
                dve.wait_ge(s_sh, r + 1)
                dve.wait_ge(s_c, 7)
                link(dve.scalar_tensor_tensor(out=cand, in0=sh, scalar=0.0, in1=over_n(em8[:, :]),
                                              op0=ALU.is_ge, op1=ALU.mult))
                link(dve.tensor_reduce(cmin, cand, axis=AX, op=ALU.min))
                dve.tensor_tensor(oh[:, 0:NT, :], over_n(em8[:, :]), over_e(cmin), ALU.is_equal)\
                    .then_inc(s_oh, 1)
                dve.wait_ge(s_ex, r + 1)
                link(dve.reduce_sum(ssum, ex, axis=AX))
                link(dve.reciprocal(ssum, ssum))
                link(dve.tensor_scalar(coef[:, :], ssum, 0.5, None, ALU.mult))
                dve.wait_ge(s_rk, r + 1)
                link(dve.tensor_copy(cnt, PS[:, 3, NT * E:NT * E + E]))
                link(dve.tensor_tensor(ntc, over_e(cnt, NT), over_n(j128[:, :], E), ALU.is_gt))
                link(dve.reduce_sum(nt, ntc, axis=AX))
                link(dve.tensor_tensor(bsm, over_n(nt, E), lower8[:, :, :], ALU.mult))
                link(dve.reduce_sum(bst, bsm, axis=AX))
                link(dve.tensor_scalar(brow, bst, float(P), None, ALU.mult))
                link(dve.tensor_tensor(bend, bst, nt, ALU.add))
                link(dve.tensor_tensor(posm, PS[:, 3, 0:NT * E].rearrange("p (n e) -> p n e", n=NT),
                                       over_n(brow), ALU.add))
                link(dve.tensor_tensor(posm, posm, oh[:, 0:NT, :], ALU.mult))
                link(dve.reduce_sum(posf, posm, axis=AX))
                dve.tensor_copy(posi[:, :], posf).then_inc(s_pos, 1)
                link(dve.tensor_tensor(mapm, over_e(slot_no[:, :]), over_n(bend, NS), ALU.is_ge))
                link(dve.reduce_sum(mapf, mapm, axis=AX))
                link(dve.tensor_scalar(mapf, mapf, float(E - 1), None, ALU.min))
                dve.tensor_copy(emap[:, :], mapf).then_inc(s_pos, 1)

            def hidden_t(r, s):
                dve.wait_ge(s_ph, s + (r * NS + 1))
                dve.tensor_copy(HT[:, ds(s & 1, 1), :], PS[:, ds((s & 1) + 2, 1), :]).then_inc(s_vh, 1)

            def slot_out(r, s):
                dve.wait_ge(s_dn, s + (r * NS + 1))
                dve.tensor_copy(YO[:, ds(s, 1), :], PS[:, ds((s & 1) + 6, 1), 0:P]).then_inc(s_y, 1)

            def constants():
                dve.wait_ge(s_b, 32)
                link(dve.tensor_copy(BT[:, 0, :], BL))
                link(dve.tensor_tensor(BR, BL, BT[:, 0, :], ALU.subtract))
                link(dve.tensor_copy(BT[:, 1, :], BR))
                link(dve.tensor_tensor(BR, BR, BT[:, 1, :], ALU.subtract))
                dve.tensor_copy(BT[:, 2, :], BR).then_inc(s_bt, 1)
                dve.wait_ge(s_c, 7)
                link(dve.tensor_scalar(MB[:, :], MB[:, :], 1, None, ALU.logical_shift_right))

            def ffn(r):
                layer_norm(2 * r, XN1)
                if r == 0:
                    constants()
                route(r)
                hidden_t(r, 0)
                with dve.Fori(1, NS) as s:
                    hidden_t(r, s)
                    slot_out(r, s - 1)
                slot_out(r, NS - 1)
                for b in range(NB):
                    dve.wait_ge(s_yg[b], 16 * TB * (r + 1))
                    for n in range(b * TB, (b + 1) * TB):
                        dve.scalar_tensor_tensor(out=X[:, n, :], in0=YG[:, n, :],
                                                 scalar=coef[:, n:n + 1], in1=X[:, n, :],
                                                 op0=ALU.mult, op1=ALU.add).then_inc(s_xr, 1)

            dve.wait_ge(s_x, 32)
            ffn(0)
            dve.wait_ge(s_xr, NT)
            layer_norm(1, XN2)

            def remainder(m):
                u, c = m // 2, m % 2
                dve.wait_ge(s_hi, m + 1)
                if m >= 2:
                    dve.wait_ge(s_lo, m - 1)
                dve.tensor_tensor(REM[:, c, :], PS[:, c, :], SP3[u][:, 0, c * SEQ:(c + 1) * SEQ],
                                  ALU.subtract).then_inc(s_rem, 1)

            def v_rows(t):
                dve.wait_ge(s_qc, t + 1)
                for k in range(2):
                    dve.tensor_copy(V[:, 2 * t + k, :, 0:HD],
                                    PS[:, 2 + t % 2, k * 2 * P + P:(k + 1) * 2 * P].rearrange(
                                        "p (h c) -> p h c", h=H)).then_inc(s_vc, 1)

            for m in range(6):
                remainder(m)
            for t in range(NT // 2):
                v_rows(t)
            for m in range(6, 12):
                remainder(m)

            def clip_scores(s, i, first):
                n = (i + 1) * P
                dve.wait_ge(s_pa, 4 * s + (i + 1))
                if not first:
                    dve.wait_ge(s_e, 8 * s + (2 * i - 2))
                bank = 2 * (i % 2)
                dve.scalar_tensor_tensor(
                    out=CL[:, i % 2, :, 0:n], in0=PS[:, bank:bank + 2, 0:n], scalar=-CLIP,
                    in1=spread(MA[:, SEQ - n:SEQ].rearrange("p (o n) -> p o n", o=1), 1, 2),
                    op0=ALU.max, op1=ALU.min).then_inc(s_cl, 1)

            def abs_scores(v, k, first):
                par, g = k // 3, k % 3
                n, at = SEG_N[g], par * HEAD_W + 512 * g
                dve.wait_ge(s_pb, 6 * v + (k + 1))
                if k == 0 and not first:
                    dve.wait_ge(s_av, v - 1)
                dve.tensor_tensor(
                    WB[:, ds(v & 1, 1), at:at + n].bitcast(i32), PS[:, 4 + k % 2:5 + k % 2, 0:n].bitcast(i32),
                    MB[:, SEG_MASK[g]:SEG_MASK[g] + n].rearrange("p (o n) -> p o n", o=1),
                    ALU.bitwise_and).then_inc(s_abs, 1)

            def heads_out(v):
                dve.wait_ge(s_aotp, (v >> 1) + 1)
                for par in range(2):
                    at = ((v >> 1) & 3) * 2 + par * HP
                    dve.tensor_copy(
                        AO[:, :, ds(at, 2), :],
                        PS[:, 6, :].rearrange("p (i e r c) -> p i e r c", i=TB, e=2, r=2)
                        [:, :, :, par, 0:HD + 1]).then_inc(s_ao, 1)

            def scale_q(b):
                dve.wait_ge(s_e, 2 * TB * HP * (b + 1))
                a = agg[:, :, :, b * HP:(b + 1) * HP].rearrange("p i par s -> p (i par) s")
                t0, s_, u_, p_, t4 = (rt[:, j, :] for j in range(5))
                link(dve.tensor_scalar(t0.rearrange('p (i s) -> p i s', s=HP), a, 2.0, 5 * EPS, ALU.mult, ALU.add))
                link(dve.tensor_scalar(t4.rearrange('p (i s) -> p i s', s=HP), a, 3 * EPS, None, ALU.add))
                link(dve.reciprocal(t0, t0))
                link(dve.reciprocal(t4, t4))
                link(dve.tensor_scalar(s_, t0, EPS, None, ALU.mult))
                link(dve.tensor_scalar(t4, t4, SCALE, None, ALU.mult))
                for i in range(TB):
                    q = QT[:, b * TB + i, :].rearrange("p (par d pair) -> p par d pair", par=2, d=HD)
                    r = spread(t4[:, i * H:(i + 1) * H].rearrange(
                        "p (par o pair) -> p par o pair", par=2, o=1), 2, HD)
                    dve.tensor_tensor(q, q, r, ALU.mult).then_inc(s_qsc, 1)
                link(dve.tensor_tensor(u_, s_, s_, ALU.mult))
                link(dve.tensor_scalar(p_, u_, 1.0 / 9.0, None, ALU.mult))
                for c in (1.0 / 7.0, 1.0 / 5.0, 1.0 / 3.0):
                    link(dve.scalar_tensor_tensor(out=p_, in0=p_, scalar=c, in1=u_,
                                                  op0=ALU.add, op1=ALU.mult))
                link(dve.scalar_tensor_tensor(out=p_, in0=p_, scalar=1.0, in1=s_,
                                              op0=ALU.add, op1=ALU.mult))
                link(dve.tensor_scalar(ckf(b), p_, 2.0, None, ALU.mult))

            def normalise(b):
                aof = AO.rearrange("p i h c -> p (i h) c")
                numf = NUM.rearrange("p i h c -> p (i h) c")
                den = rt[:, 0, :]
                dve.wait_ge(s_ao, HP * (b + 1))
                dve.wait_ge(s_cv, b + 1)
                link(dve.tensor_tensor(numf, PS[:, 7, :].rearrange("p (h c) -> p h c", c=HD),
                                       over_e(ckf(b), HD), ALU.mult))
                link(dve.tensor_tensor(numf, numf, aof[:, :, 0:HD], ALU.add))
                link(dve.tensor_tensor(den.rearrange("p (i h) -> p i h", i=TB), ck[:, b % 2, :, :],
                                       over_e(seen[:, :], H), ALU.mult))
                link(dve.tensor_tensor(den, den, aof[:, :, HD], ALU.add))
                link(dve.tensor_scalar(den, den, EPS, None, ALU.add))
                link(dve.reciprocal(den, den))
                dve.tensor_tensor(numf, numf, over_e(den, HD), ALU.mult).then_inc(s_num, 1)

            breaks = [b * HP + k for b in range(NB) for k in (R_AT, Q_AT, N_AT, X_AT)]
            dve.wait_ge(s_lo, 12)
            for s0, s1 in stretches(breaks):
                with steps(dve, s0, s1) as base:
                    for odd in range(2):
                        s, v = base + odd, base + (odd - LAG)
                        for k in range(6):
                            if s0 < STEPS and k < TB:
                                clip_scores(s, k, s0 == 0 and not odd and k < 2)
                            if LAG <= s0 < STEPS + LAG:
                                abs_scores(v, k, s0 == LAG)
                        if odd and LAG + 2 <= s0 < LAST_STEP:
                            heads_out(v - 3)
                for b in range(NB):
                    if s1 == b * HP + R_AT + 1:
                        scale_q(b)
                    if s1 == b * HP + Q_AT + 1:
                        dve.wait_ge(s_qhi, b + 1)
                        if b:
                            dve.wait_ge(s_qlo, b)
                        dve.tensor_tensor(QREM, PS[:, 7, :], QP3[:, 0, :], ALU.subtract)\
                            .then_inc(s_qrem, 1)
                    if s1 == b * HP + N_AT + 1:
                        normalise(b)
                    if s1 == b * HP + X_AT + 1:
                        dve.wait_ge(s_pr, b + 1)
                        xb = X[:, b * TB:(b + 1) * TB, :]
                        dve.tensor_tensor(xb, PS[:, 7, :].rearrange("p (n d) -> p n d", n=TB), xb,
                                          ALU.add).then_inc(s_xr, 1)
            dve.wait_ge(s_xr, NT + NB)
            ffn(1)

        @block.tensor
        def _(pe):
            def layer_norm(k, xn):
                for g in range(NB):
                    pe.wait_ge(s_xn, NT * k + TB * (g + 1))
                    if g >= 2:
                        pe.wait_ge(s_xnt, NB * k + g - 1)
                    for j in range(TB):
                        last = pe.transpose(PS[:, g % 2, j * P:(j + 1) * P], xn[:, g * TB + j, :],
                                            ident[:, :])
                    last.then_inc(s_tp, 1)

            def route(r):
                pe.wait_ge(s_xnt, NB * (2 * r + 1))
                for n in range(NT):
                    last = pe.matmul(PS[:, 2, n * E:(n + 1) * E], XNT1[:, n * P:(n + 1) * P], WG[:, :],
                                     start=True, stop=True)
                last.then_inc(s_sc, 1)
                pe.wait_ge(s_oh, r + 1)
                pe.matmul(PS[:, 3, 0:(NT + 1) * E], utri[:, :], oh, start=True, stop=False)
                for n in range(NT):
                    last = pe.matmul(PS[:, 3, (n + 1) * E:(NT + 1) * E], onesb[:, :],
                                     spread(oh[:, n:n + 1, :], 1, NT - n), start=False, stop=n == NT - 1)
                last.then_inc(s_rk, 1)

            def slot_transposes(r, g):
                pe.wait_ge(s_xs[r][g], 16)
                if g >= 2:
                    pe.wait_ge(s_vx, r * GROUPS + g - 1)
                for s in range(4 * g, min(4 * g + 4, NS)):
                    last = pe.transpose(PS[:, 4 + g % 2, (s % 4) * P:(s % 4 + 1) * P], XS[:, s, :],
                                        ident[:, :])
                last.then_inc(s_px, 1)

            def up(r, s, e):
                if s % 4 == 0:
                    pe.wait_ge(s_vx, r * GROUPS + s // 4 + 1)
                if s >= 2:
                    pe.wait_ge(s_h, r * NS + s - 1)
                pe.matmul(PS[:, s % 2, :], XT[:, s // 4 % 2, (s % 4) * P:(s % 4 + 1) * P],
                          W1[:, ds(e * F, F)], start=True, stop=False)
                pe.matmul(PS[:, s % 2, :], onesb[0:TERMS, :], BS[:, ds(e * (F + P), F)],
                          start=False, stop=True).then_inc(s_up, 1)

            def hidden_t(r, s):
                pe.wait_ge(s_h, r * NS + s + 1)
                if s >= 2:
                    pe.wait_ge(s_vh, r * NS + s - 1)
                for c in range(FC):
                    last = pe.transpose(PS[:, 2 + s % 2, c * P:(c + 1) * P],
                                        HB[:, s % 2, c * P:(c + 1) * P], ident[:, :])
                last.then_inc(s_ph, 1)

            def down(r, s, e):
                pe.wait_ge(s_vh, r * NS + s + 1)
                if s >= 2:
                    pe.wait_ge(s_y, r * NS + s - 1)
                for c in range(FC):
                    pe.matmul(PS[:, 6 + s % 2, 0:P], HT[:, s % 2, c * P:(c + 1) * P],
                              W2[:, ds(e * F + c * P, P)], start=c == 0, stop=False)
                pe.matmul(PS[:, 6 + s % 2, 0:P], onesb[0:TERMS, :], BS[:, ds(e * (F + P) + F, P)],
                          start=False, stop=True).then_inc(s_dn, 1)

            def ffn(r):
                layer_norm(2 * r, XN1)
                route(r)
                pe.wait_ge(s_pos, 2 * r + 2)
                pe.wait_ge(s_w, 32 * (r + 1))
                pe.wait_ge(s_bs, 16 * (r + 1))
                expert = {}
                slot_transposes(r, 0)
                for s in range(NS + 2):
                    if s < NS:
                        expert[s] = pe.value_load(emap[0:1, s:s + 1], min_val=0, max_val=E - 1)
                        up(r, s, expert[s])
                        if s % 4 == 1 and s // 4 + 1 < GROUPS:
                            slot_transposes(r, s // 4 + 1)
                    if 1 <= s <= NS:
                        hidden_t(r, s - 1)
                    if s >= 2:
                        down(r, s - 2, expert.pop(s - 2))

            pe.wait_ge(s_c, 7)
            pe.wait_ge(s_x, 32)
            ffn(0)
            layer_norm(1, XN2)
            pe.wait_ge(s_wa, 16)
            pe.wait_ge(s_xnt, 2 * NB)

            def project(m):
                which, w = UNITS[m // 2]
                if m >= 2:
                    pe.wait_ge(s_hi, m - 1)
                    pe.wait_ge(s_rem, m - 1)
                at = w * 2 * SEQ + (m % 2) * SEQ
                pe.matmul(PS[:, m % 2, :], WA[:, WCOL[which], :], XNT2[:, at:at + SEQ],
                          start=True, stop=True).then_inc(s_pj, 1)

            def q_v_rows(t):
                if t >= 2:
                    pe.wait_ge(s_qc, t - 1)
                    pe.wait_ge(s_vc, 2 * (t - 1))
                for k in range(2):
                    n = 2 * t + k
                    last = pe.matmul(PS[:, 2 + t % 2, k * 2 * P:(k + 1) * 2 * P],
                                     XNT2[:, n * P:(n + 1) * P], WA[:, 0:2, :], start=True, stop=True)
                last.then_inc(s_qv, 1)

            for m in range(6):
                project(m)
            for t in range(NT // 2):
                q_v_rows(t)
            for m in range(6, 12):
                project(m)

            def scores_a(s, i):
                b, hp, n = s // HP, s % HP, (i + 1) * P
                a = 4 * s + i
                if a >= 2:
                    pe.wait_ge(s_cl, a - 1)
                for par in range(2):
                    rows = slice(64 * par, 64 * par + KROWS)
                    last = pe.matmul(PS[:, 2 * (i % 2) + par, 0:n],
                                     QS[rows, hp, (b * TB + i) * P:(b * TB + i + 1) * P],
                                     YS[rows, hp, b * SEQ:b * SEQ + n], start=True, stop=True)
                last.then_inc(s_pa, 1)

            def scores_b(v, k):
                b, hp, par, g = v // HP, v % HP, k // 3, k % 3
                c = 6 * v + k
                if c >= 2:
                    pe.wait_ge(s_abs, c - 1)
                rows = slice(64 * par, 64 * par + KROWS)
                at = 0
                for j in SEG_J[g]:
                    n = SEQ - j * P
                    last = pe.matmul(PS[:, 4 + k % 2, at:at + n],
                                     KS[rows, hp, (b * TB + j) * P:(b * TB + j + 1) * P],
                                     QPS[rows, b % 2, hp, j * P:SEQ], start=True, stop=True)
                    at += n
                last.then_inc(s_pb, 1)

            def weigh(v):
                b, hp = v // HP, v % HP
                pe.wait_ge(s_ln, v + 1)
                if v >= 2:
                    pe.wait_ge(s_ao, v // 2 * 2)
                for j in range(TB):
                    for par in range(2):
                        quad = QUAD * (2 * (v % 2) + par)
                        at = par * HEAD_W + J_OFF[j]
                        head = ((b * TB + j) * H + par * HP + hp) * (HD + 1)
                        last = pe.matmul(PS[quad:quad + QUAD, 6, j * P:SEQ], VF[:, head:head + QUAD],
                                         WB[:, v % 2, at:at + SEQ - j * P],
                                         start=j == 0, stop=j == TB - 1)
                last.then_inc(s_av, 1)

            def weighed_t(v):
                pe.wait_ge(s_aot, v // 2 + 1)
                for i in range(TB):
                    last = pe.transpose(PS[:, 6, i * P:(i + 1) * P], AOT[:, i * P:(i + 1) * P],
                                        ident[:, :])
                last.then_inc(s_aotp, 1)

            def after(s):
                for b in range(NB):
                    at = s - b * HP
                    if at == Q_AT:
                        pe.wait_ge(s_qsc, TB * (b + 1))
                        if b >= 2:
                            pe.wait_ge(s_xr, NT + b - 1)
                        for i in range(TB):
                            last = pe.transpose(PS[:, 7, i * P:(i + 1) * P], QT[:, b * TB + i, :],
                                                ident[:, :])
                        last.then_inc(s_qt, 1)
                    if at == C_AT:
                        if b + 1 < NB:
                            pe.wait_ge(s_qhi, b + 2)
                            pe.wait_ge(s_qrem, b + 2)
                        if b:
                            pe.wait_ge(s_xr, NT + b)
                        for i in range(TB):
                            for j in range(i + 1):
                                last = pe.matmul(PS[:, 7, i * P:(i + 1) * P],
                                                 (tri if j == i else ones)[:, :],
                                                 V[:, b * TB + j, :, 0:HD], start=j == 0, stop=j == i)
                        last.then_inc(s_cv, 1)
                    if at == T_AT:
                        pe.wait_ge(s_num, b + 1)
                        for i in range(TB):
                            last = pe.transpose(PS[:, 7, i * P:(i + 1) * P],
                                                NUM[:, i, :, :].rearrange("p h c -> p (h c)"), ident[:, :])
                        last.then_inc(s_ot, 1)
                    if at == P_AT:
                        pe.wait_ge(s_otc, b + 1)
                        for i in range(TB):
                            last = pe.matmul(PS[:, 7, i * P:(i + 1) * P], OT[:, i * P:(i + 1) * P],
                                             WA[:, 4, :], start=True, stop=True)
                        last.then_inc(s_pr, 1)

            pe.wait_ge(s_hi, 12)
            pe.wait_ge(s_rem, 12)
            pe.wait_ge(s_qc, NT // 2)
            pe.wait_ge(s_vc, NT)
            for s in range(END_STEP):
                v = s - LAG
                for u, (which, w) in enumerate(UNITS):
                    if (v if which == 2 else s) == w * 2 * HP:
                        pe.wait_ge(s_stk[u], STACK_DMAS)
                if 0 <= v < STEPS and v % HP == 0:
                    pe.wait_ge(s_qps, STACK_DMAS * (v // HP + 1))
                for k in range(6):
                    if s < STEPS and k < TB:
                        scores_a(s, k)
                    if 0 <= v < STEPS:
                        scores_b(v, k)
                    if k == 3 and v % 2 and 3 <= v <= STEPS + 1:
                        weighed_t(v - 3)
                if 1 <= v <= STEPS:
                    weigh(v - 1)
                after(s)
            ffn(1)


def kernel(L0_attn_x, L0_attn_w_qkv, L0_attn_w_ky, L0_attn_w_proj, L0_ffn_Wg, L0_ffn_W1, L0_ffn_b1,
           L0_ffn_W2, L0_ffn_b2):
    import concourse.bacc as bacc
    from concourse.bass_utils import run_bass_kernel_spmd

    def c(a):
        return np.ascontiguousarray(a)

    wq, wk, wv = np.split(np.asarray(L0_attn_w_qkv), 3, axis=0)

    def by_channel(w):
        return np.transpose(np.asarray(w).reshape(HP, 2, HD, P), (1, 2, 0, 3)).reshape(P, P).T

    def by_head(w):
        return np.transpose(np.asarray(w).reshape(HP, 2, HD, P), (1, 0, 2, 3)).reshape(P, P).T

    proj = np.transpose(np.asarray(L0_attn_w_proj).reshape(P, HP, 2, HD), (2, 1, 3, 0)).reshape(P, P)
    wattn = np.stack([by_channel(wq), by_head(wv), by_channel(L0_attn_w_ky), by_channel(wk), proj], 1)
    arrays = {
        "x": c(np.asarray(L0_attn_x).reshape(NT * P, P)),
        "wattn": c(wattn),
        "wg": c(np.asarray(L0_ffn_Wg).T),
        "w1": c(np.transpose(np.asarray(L0_ffn_W1), (2, 0, 1)).reshape(P, E * F)),
        "b1": c(L0_ffn_b1),
        "w2": c(np.transpose(np.asarray(L0_ffn_W2).reshape(E, P, FC, P), (3, 0, 2, 1)).reshape(P, E * F)),
        "b2": c(L0_ffn_b2),
    }
    nc = bacc.Bacc("TRN2", target_bir_lowering=False, num_devices=1)
    args = [nc.dram_tensor(n, a.shape, mybir.dt.from_np(a.dtype), kind="ExternalInput").ap()
            for n, a in arrays.items()]
    out = nc.dram_tensor("out", (NT * P, P), mybir.dt.float32, kind="ExternalOutput").ap()
    build(nc, *args, out)
    r = run_bass_kernel_spmd(nc, [arrays], core_ids=[0])
    return r.results[0]["out"].reshape(NB, SEQ, P)
```

```python
import numpy as np
import concourse.bass as bass
from concourse import mybir
from contextlib import ExitStack, contextmanager

P = 128
NT = 16
NB, TB = 4, 4
SEQ = TB * P
E, F = 8, 512
FC = F // P
W1_W = F + FC
RING = 4
NS = NT + E - 1
H, HD = 16, 8
HP = H // 2
TERMS = 3
Q_TERMS = (0, 0, 1, 1, 0, 2)
K_TERMS = (0, 1, 0, 1, 2, 0)
KROWS = HD * len(Q_TERMS)
EXP_AND_LN = 6
EPS = 1e-6
LN_EPS = 1e-5
SCALE = float(1.0 / np.sqrt(HD))
CLIP = 15.0 / SCALE
MASKED = -3.0e4
STEPS = NB * HP
LAG = HP + 4
SEG_J = ((0,), (3, 1), (2,))
SEG_N = (512, 512, 256)
SEG_MASK = (128, 0, 128)
QUAD = 32
WEIGH_TILES = ((0,), (1,), (2, 3))
AO_BANK, AO_K, AO_COL = 5, 5, 256
J_OFF = {0: 0, 3: 512, 1: 640, 2: 1024}
HEAD_W = 1280
STACK_DMAS = 16 * 2 * len(Q_TERMS)
GROUPS = -(-NS // 4)
A_AT = HP - 1
R_AT = A_AT + 1
Q_AT = R_AT + 1
C_AT = LAG + HP - 1
V_AT = C_AT + 1
N_AT = LAG + HP + 1
T_AT = N_AT + 1
P_AT = T_AT + 1
X_AT = P_AT + 1
LAST_STEP = STEPS + LAG + 2
END_STEP = (NB - 1) * HP + X_AT + 2


def stretches(stages):
    cuts = {0, 2, LAG, LAG + 2, LAG + 4, STEPS, STEPS + LAG, LAST_STEP, END_STEP}
    for at in stages:
        for b in range(NB):
            s = (b * HP + at) // 2 * 2
            cuts |= {s, s + 2}
    cuts = sorted(c for c in cuts if c <= END_STEP)
    return list(zip(cuts[:-1], cuts[1:]))


@contextmanager
def steps(engine, s0, s1):
    if s1 - s0 == 2 or s0 >= LAST_STEP:
        yield s0
    else:
        with engine.Fori(s0 // 2, s1 // 2) as m:
            yield m * 2


def build(nc, x_in, wattn_in, wg_in, w1_in, w2_in, b2_in, out):
    f32, bf16, u32, i32 = mybir.dt.float32, mybir.dt.bfloat16, mybir.dt.uint32, mybir.dt.int32
    ALU, ACT, AX = mybir.AluOpType, mybir.ActivationFunctionType, mybir.AxisListType.X
    ds = bass.ds
    ctx = ExitStack()
    with ctx:
        def sb(name, shape, dt=f32):
            return ctx.enter_context(nc.sbuf_tensor(name, shape, dt))

        def sem(name):
            return ctx.enter_context(nc.semaphore(name))

        X = sb("X", [P, NT, P])
        R1 = sb("R1", [P, 8192])
        W1 = R1[:, 0:RING * W1_W].rearrange("p (r n) -> p r n", r=RING)
        W2 = R1[:, RING * W1_W:RING * W1_W + E * F]
        XN2 = R1[:, 0:2048].rearrange("p (n d) -> p n d", n=NT)
        XNT2 = R1[:, 2048:4096]
        REM = R1[:, 4096:5120].rearrange("p (r n) -> p r n", r=2)
        WB = R1[:, 0:5120].rearrange("p (r n) -> p r n", r=2)
        QP3 = R1[:, 5120:5888].bitcast(bf16).rearrange("p (t n) -> p t n", t=TERMS)
        AOT = R1[:, 5888:6400]
        AO = R1[:, 6400:6976].rearrange("p (i h c) -> p i h c", i=TB, h=H)
        NUM = R1[:, 6976:7488].rearrange("p (i h c) -> p i h c", i=TB, h=H)
        OT = R1[:, 7488:8000]
        QREM = OT
        stats = R1[:, 8000:8096].rearrange("p (n s) -> p n s", n=NT)
        mv = R1[:, 8096:8128].rearrange("p (n s) -> p n s", n=NT)
        lnt = R1[:, 8128:8192].rearrange("p (k n) -> p k n", k=4)
        R2 = sb("R2", [P, 4608])
        XN1 = R2[:, 0:2048].rearrange("p (n d) -> p n d", n=NT)
        XNT1 = R2[:, 2048:4096]
        R2B = R2[:, :].bitcast(bf16).rearrange("p (r t n) -> p r t n", r=3, t=TERMS)
        R3 = sb("R3", [P, 24576])
        stacks = R3[:, :].bitcast(bf16).rearrange("p (s q n) -> p s q n", s=3, q=HP)
        QS, YS, KS = stacks[:, 0], stacks[:, 1], stacks[:, 2]
        XS = R3[:, 0:NS * P].rearrange("p (s d) -> p s d", s=NS)
        YO = R3[:, 2944:2944 + NS * P].rearrange("p (s d) -> p s d", s=NS)
        YG = R3[:, 5888:7936].rearrange("p (n d) -> p n d", n=NT)
        HT = R3[:, 8960:9984].rearrange("p (r n) -> p r n", r=2)
        BS = R3[0:TERMS, 9984:10496].bitcast(bf16)
        BL = R3[0:E, 12544:12672]
        BR = R3[0:E, 12672:12800]
        BT = R3[0:E, 13824:14016].bitcast(bf16).rearrange("p (t n) -> p t n", t=TERMS)
        XT = R3[:, 14784:15808].rearrange("p (r n) -> p r n", r=2)
        T3 = R3[:, 16384:24576]
        sh = T3[:, 0:128].rearrange("p (n e) -> p n e", n=NT)
        ex = T3[:, 128:256].rearrange("p (n e) -> p n e", n=NT)
        cand = T3[:, 256:384].rearrange("p (n e) -> p n e", n=NT)
        posm = T3[:, 384:512].rearrange("p (n e) -> p n e", n=NT)
        ntc = T3[:, 512:640].rearrange("p (e j) -> p e j", e=E)
        bsm = T3[:, 640:704].rearrange("p (e j) -> p e j", e=E)
        mapm = T3[:, 704:704 + NS * E].rearrange("p (s e) -> p s e", s=NS)
        rt = sb("rt", [P, 6, TB * H])
        mx, cmin, ssum, posf = (T3[:, 896 + 16 * k:912 + 16 * k] for k in range(4))
        cnt, nt, bst, brow, bend = (T3[:, 960 + 8 * k:968 + 8 * k] for k in range(5))
        mapf = T3[:, 1000:1000 + NS]
        oh = T3[:, 1024:1092].bitcast(bf16).rearrange("p (n e) -> p n e", n=NT + 1)
        QT = sb("QT", [P, NT, P])
        VF = sb("V", [P, NT * H * (HD + 1) + QUAD])
        V = VF[:, 0:NT * H * (HD + 1)].rearrange("p (n h c) -> p n h c", n=NT, h=H)
        QPS = sb("QPS", [P, 2, HP, SEQ], bf16)
        QB = QPS[:, :, :, :].rearrange("p r q n -> p (r q n)")[:, 0:2 * TERMS * 2 * SEQ]\
            .rearrange("p (r t n) -> p r t n", r=2, t=TERMS)
        SP3 = (R2B[:, 0], R2B[:, 1], R2B[:, 2], QB[:, 0], QB[:, 1], R2B[:, 0])
        CL3 = sb("CL3", [P, 2, SEQ])
        CL = [R2[:, 1536 + a:1536 + a + 2 * n].rearrange("p (r n) -> p r n", r=2)
              for a, n in ((0, P), (2 * P, 2 * P), (6 * P, 3 * P))] + [CL3]
        WA = sb("WA", [P, 5, P])
        WG = sb("WG", [P, E])
        ident = sb("ident", [P, P])
        tri = sb("tri", [P, P])
        ones = sb("ones", [P, P])
        MA = sb("MA", [P, SEQ])
        MB = sb("MB", [P, 5 * P], i32)
        utri = sb("utri", [P, P], bf16)
        onesb = sb("onesb", [P, P], bf16)
        em8 = sb("em8", [P, E])
        j128 = sb("j128", [P, NT])
        lower8 = sb("lower8", [P, E, E])
        slot_no = sb("slot_no", [P, NS])
        seen = sb("seen", [P, TB])
        agg = sb("agg", [P, TB, 2, STEPS])
        ck = sb("ck", [P, 2, TB, H])
        coef = sb("coef", [P, NT])
        posi = sb("posi", [P, NT], u32)
        emap = sb("emap", [P, NS], u32)
        PS = ctx.enter_context(nc.psum_tensor("PS", [P, 8, 512], f32))
        xs_d = nc.dram_tensor("xs_d", (NS * P, P), f32, kind="Internal").ap()
        ys_d = nc.dram_tensor("ys_d", (NS * P, P), f32, kind="Internal").ap()
        bs_d = nc.dram_tensor("bias_terms_d", (TERMS, E * P), bf16, kind="Internal").ap()

        s_x = [sem(f"x_{b}_loaded") for b in range(NB)]
        s_wg = sem("gate_weights_loaded")
        s_wa = sem("attn_weights_loaded")
        s_w1 = [sem(f"w1_ring_{k}_loaded") for k in range(RING)]
        s_w2 = sem("w2_loaded")
        s_b = sem("biases_loaded")
        s_bt = sem("bias_terms_ready")
        s_bd = sem("bias_terms_stored")
        s_bs = sem("bias_rows_loaded")
        s_z = sem("zero_tile_ready")
        s_zd = sem("scratch_zeroed")
        s_c0 = sem("const_fill")
        s_c = sem("consts_ready")
        s_dve = sem("dve_chain")
        s_var = sem("variance_ready")
        s_std = sem("std_ready")
        s_xn = sem("xn_ready")
        s_tp = sem("xnt_transposed")
        s_xnt = sem("xnt_copied")
        s_sc = sem("scores_ready")
        s_sh = sem("shifted_scores")
        s_ex = sem("exp_scores")
        s_oh = sem("onehot_ready")
        s_rk = sem("ranks_ready")
        s_pos = sem("positions_ready")
        s_sct = sem("rows_scattered")
        s_xs = [[sem(f"slots_{r}_{g}_loaded") for g in range(GROUPS)] for r in range(2)]
        s_px = sem("slot_transposed")
        s_vx = sem("slot_t_copied")
        s_up = sem("up_done")
        s_h = sem("gelu_done")
        s_dn = sem("down_done")
        s_y = sem("y_copied")
        s_yd = sem("y_stored")
        s_yg = [sem(f"y_{b}_gathered") for b in range(NB)]
        s_xr = sem("residual_ready")
        s_pj = sem("projection_done")
        s_hi = sem("first_term_ready")
        s_rem = sem("remainder_ready")
        s_lo = sem("terms_ready")
        s_mid = sem("second_term_ready")
        s_stk = [sem(f"stack_{i}_written") for i in range(6)]
        s_qv = sem("qv_done")
        s_qc = sem("q_copied")
        s_vc = sem("v_copied")
        s_pa = sem("ly_ready")
        s_cl = sem("clipped")
        s_e = sem("exp_summed")
        s_qsc = sem("q_scaled")
        s_qt = sem("scaled_q_transposed")
        s_qhi = sem("scaled_q_first_term")
        s_qrem = sem("scaled_q_remainder")
        s_qmid = sem("scaled_q_second_term")
        s_qlo = sem("scaled_q_terms_ready")
        s_qps = sem("scaled_q_stacked")
        s_pb = sem("l_ready")
        s_abs = sem("abs_done")
        s_ln = sem("ln_done")
        s_av = sem("av_done")
        s_aot = sem("av_out_of_psum")
        s_aotp = sem("av_transposed")
        s_ao = sem("av_copied")
        s_cv = sem("v_prefix_done")
        s_pool = sem("pool_chain")
        s_apre = sem("agg_sums_ready")
        s_arec = sem("agg_reciprocals_ready")
        s_dpre = sem("denominator_part_ready")
        s_drec = sem("denominator_reciprocal_ready")
        s_ck = sem("ck_ready")
        s_vp = sem("v_prefix_scaled")
        s_num = sem("attn_out_ready")
        s_ot = sem("attn_out_transposed")
        s_otc = sem("attn_out_t_copied")
        s_pr = sem("attn_projected")
        s_out = sem("output_stored")

        aggf = agg[:, :, :, :].rearrange("p i par s -> p (i par s)")
        UNITS = ((0, 0), (1, 0), (2, 0), (0, 1), (1, 1), (2, 1))
        WCOL = (0, 2, 3)

        def stack_rows(par, t):
            return slice(64 * par + HD * t, 64 * par + HD * t + HD)

        def half(w):
            return slice(w * 2 * SEQ, (w + 1) * 2 * SEQ)

        def spread(a, axis, n):
            shape = list(a.shape)
            shape[axis] = n
            return a.broadcast_to(shape)

        def ckf(b):
            return ck[:, b % 2, :, :].rearrange("p i h -> p (i h)")

        block = ctx.enter_context(nc.Block())


        @block.sync
        def _(sp):
            for b in range(NB):
                sp.dma_start(X[:, b * TB:(b + 1) * TB, :],
                             x_in[b * SEQ:(b + 1) * SEQ, :].rearrange("(n p) d -> p n d", p=P))\
                    .then_inc(s_x[b], 16)
            sp.dma_start(WG[:, :], wg_in).then_inc(s_wg, 16)
            sp.dma_start(BL, b2_in).then_inc(s_b, 16)
            sp.wait_ge(s_z, 1)
            sp.dma_start(xs_d.rearrange("(s p) d -> p s d", p=P), XS).then_inc(s_zd, 16)
            sp.dma_start(W2, w2_in).then_inc(s_w2, 16)
            sp.dma_start(WA[:, :, :], wattn_in).then_inc(s_wa, 16)
            sp.wait_ge(s_bt, 1)
            sp.dma_start(bs_d.rearrange("t (e n) -> e t n", e=E), BT).then_inc(s_bd, 16)
            sp.wait_ge(s_bd, 16)
            sp.dma_start(BS, bs_d).then_inc(s_bs, 16)

            def load_w1(r, s, k, first):
                e = sp.value_load(emap[0:1, s:s + 1] if first else emap[0:1, ds(s, 1)],
                                  min_val=0, max_val=E - 1)
                if not first:
                    sp.wait_ge(s_h, s + (r * NS - RING + 1))
                sp.dma_start(W1[:, k, :], w1_in[ds(e, 1), :, :].rearrange("o p n -> p (o n)"))\
                    .then_inc(s_w1[k], 16)

            def store_y(r, s):
                sp.wait_ge(s_y, s + (r * NS + 1))
                sp.dma_start(ys_d[ds(s * P, P), :], YO[:, ds(s, 1), :]).then_inc(s_yd, 16)

            def slots(r):
                sp.wait_ge(s_pos, 2 * r + 2)
                for k in range(RING):
                    load_w1(r, k, k, True)
                sp.wait_ge(s_sct, 16 * NT * (r + 1))
                for g in range(0, NS, 4):
                    s1 = min(g + 4, NS)
                    sp.dma_start(XS[:, g:s1, :],
                                 xs_d[g * P:s1 * P, :].rearrange("(s p) d -> p s d", p=P))\
                        .then_inc(s_xs[r][g // 4], 16)
                with sp.Fori(0, NS // RING - 1) as g:
                    for k in range(RING):
                        load_w1(r, g * RING + (RING + k), k, False)
                        store_y(r, g * RING + k)
                done = (NS // RING - 1) * RING
                for k in range(NS % RING):
                    load_w1(r, done + RING + k, k, False)
                for s in range(done, NS):
                    store_y(r, s)

            slots(0)
            for u, (which, w) in enumerate(UNITS):
                sp.wait_ge(s_lo, 2 * (u + 1))
                dst = (QS, YS, KS)[which]
                for t, term in enumerate(K_TERMS if which else Q_TERMS):
                    for par in range(2):
                        sp.dma_start(dst[stack_rows(par, t), :, half(w)],
                                     SP3[u][64 * par:64 * par + 64, term, :]).then_inc(s_stk[u], 16)
            sp.wait_ge(s_stk[3], STACK_DMAS)
            sp.wait_ge(s_stk[4], STACK_DMAS)
            for b in range(NB):
                sp.wait_ge(s_qlo, b + 1)
                if b >= 2:
                    sp.wait_ge(s_pb, 6 * HP * (b - 1))
                for t, term in enumerate(Q_TERMS):
                    for par in range(2):
                        sp.dma_start(QPS[stack_rows(par, t), b % 2, :, :],
                                     QP3[64 * par:64 * par + 64, term, :]).then_inc(s_qps, 16)
            sp.wait_ge(s_pb, 6 * STEPS)
            sp.dma_start(BS, bs_d).then_inc(s_bs, 16)
            sp.wait_ge(s_pr, NB)
            sp.dma_start(W2, w2_in).then_inc(s_w2, 16)
            slots(1)
            for b in range(NB):
                sp.wait_ge(s_xr, NT + NB + TB * (b + 1))
                sp.dma_start(out[b * SEQ:(b + 1) * SEQ, :].rearrange("(n p) d -> p n d", p=P),
                             X[:, b * TB:(b + 1) * TB, :]).then_inc(s_out, 16)
            sp.wait_ge(s_out, 16 * NB)

        @block.gpsimd
        def _(pool):
            pool.memset(XS, 0.0).then_inc(s_z, 1)
            pool.memset(ident[:, :], 0.0).then_inc(s_c0, 1)
            pool.memset(tri[:, :], 1.0).then_inc(s_c0, 1)
            pool.memset(ones[:, :], 1.0).then_inc(s_c0, 1)
            pool.memset(utri[:, :], 1.0).then_inc(s_c0, 1)
            pool.memset(onesb[:, :], 1.0).then_inc(s_c0, 1)
            pool.memset(MA[:, :], CLIP).then_inc(s_c0, 1)
            pool.memset(MB[:, :], -1).then_inc(s_c0, 1)
            pool.memset(VF[:, :], 1.0).then_inc(s_c0, 1)
            ok = dict(allow_small_or_imprecise_dtypes=True)
            pool.iota(em8[:, :], [[1, E]], base=-E, channel_multiplier=0, **ok).then_inc(s_c0, 1)
            pool.iota(j128[:, :], [[P, NT]], base=0, channel_multiplier=0, **ok).then_inc(s_c0, 1)
            pool.iota(lower8[:, :, :], [[1, E], [-1, E]], base=0, channel_multiplier=0, **ok)\
                .then_inc(s_c0, 1)
            pool.iota(slot_no[:, :], [[1, NS]], base=0, channel_multiplier=0, **ok).then_inc(s_c0, 1)
            pool.iota(seen[:, :], [[P, TB]], base=1, channel_multiplier=1, **ok).then_inc(s_c0, 1)
            pool.wait_ge(s_c0, 13)
            pool.affine_select(out=ident[:, :], in_=ident[:, :], compare_op=ALU.not_equal, fill=1.0,
                               base=0, pattern=[[-1, P]], channel_multiplier=1).then_inc(s_c, 1)
            pool.affine_select(out=tri[:, :], in_=tri[:, :], compare_op=ALU.is_ge, fill=0.0,
                               base=0, pattern=[[1, P]], channel_multiplier=-1).then_inc(s_c, 1)
            pool.affine_select(out=utri[:, :], in_=utri[:, :], compare_op=ALU.is_gt, fill=0.0,
                               base=0, pattern=[[1, P]], channel_multiplier=-1).then_inc(s_c, 1)
            pool.affine_select(out=MA[:, SEQ - P:SEQ], in_=MA[:, SEQ - P:SEQ], compare_op=ALU.is_ge,
                               fill=MASKED, base=0, pattern=[[-1, P]], channel_multiplier=1)\
                .then_inc(s_c, 1)
            for at in (0, P):
                pool.affine_select(out=MB[:, at:at + P], in_=MB[:, at:at + P], compare_op=ALU.is_ge,
                                   fill=0, base=0, pattern=[[1, P]], channel_multiplier=-1)\
                    .then_inc(s_c, 1)
            pool.tensor_scalar(lower8[:, :, :], lower8[:, :, :], 0.0, None, ALU.is_gt).then_inc(s_c, 1)

            def scatter(r):
                pool.wait_ge(s_pos, 2 * r + 1)
                if r == 0:
                    pool.wait_ge(s_zd, 16)
                for n in range(NT):
                    pool.indirect_dma_start(xs_d, bass.IndirectOffsetOnAxis(posi[:, n:n + 1], 0),
                                            XN1[:, n, :], None).then_inc(s_sct, 16)

            def gather(r):
                pool.wait_ge(s_yd, 16 * NS * (r + 1))
                for n in range(NT):
                    pool.indirect_dma_start(YG[:, n, :], None, ys_d,
                                            bass.IndirectOffsetOnAxis(posi[:, n:n + 1], 0))\
                        .then_inc(s_yg[n // TB], 16)

            scatter(0)
            gather(0)
            for u in range(len(UNITS)):
                for c in range(2):
                    m = 2 * u + c
                    pool.wait_ge(s_mid, m + 1)
                    pool.tensor_tensor(SP3[u][:, 2, c * SEQ:(c + 1) * SEQ], REM[:, c, :],
                                       SP3[u][:, 1, c * SEQ:(c + 1) * SEQ], ALU.subtract)\
                        .then_inc(s_lo, 1)
            done = [0]

            def link(ins):
                done[0] += 1
                ins.then_inc(s_pool, 1)
                pool.wait_ge(s_pool, done[0])

            def agg_sums(b):
                pool.wait_ge(s_e, 2 * TB * HP * (b + 1))
                a = agg[:, :, :, b * HP:(b + 1) * HP].rearrange("p i par s -> p (i par) s")
                by_pair = [rt[:, k, :].rearrange("p (i s) -> p i s", s=HP) for k in range(2)]
                link(pool.tensor_scalar(by_pair[0], a, 2.0, 5 * EPS, ALU.mult, ALU.add))
                pool.tensor_scalar(by_pair[1], a, 3 * EPS, None, ALU.add).then_inc(s_apre, 1)

            def scale_q(b):
                t0, t4, s_, u_, p_, den = (rt[:, j, :] for j in range(6))
                pool.wait_ge(s_arec, b + 1)
                link(pool.tensor_scalar(t4, t4, SCALE, None, ALU.mult))
                for i in range(TB):
                    q = QT[:, b * TB + i, :].rearrange("p (par d pair) -> p par d pair", par=2, d=HD)
                    r = spread(t4[:, i * H:(i + 1) * H].rearrange(
                        "p (par o pair) -> p par o pair", par=2, o=1), 2, HD)
                    pool.tensor_tensor(q, q, r, ALU.mult).then_inc(s_qsc, 1)
                link(pool.tensor_scalar(s_, t0, EPS, None, ALU.mult))
                link(pool.tensor_tensor(u_, s_, s_, ALU.mult))
                link(pool.tensor_scalar(p_, u_, 1.0 / 9.0, 1.0 / 7.0, ALU.mult, ALU.add))
                for c in (1.0 / 5.0, 1.0 / 3.0, 1.0):
                    link(pool.tensor_tensor(p_, p_, u_, ALU.mult))
                    link(pool.tensor_scalar(p_, p_, c, None, ALU.add))
                link(pool.tensor_tensor(p_, p_, s_, ALU.mult))
                pool.tensor_scalar(ckf(b), p_, 2.0, None, ALU.mult).then_inc(s_ck, 1)

            def key_counts(b):
                pool.wait_ge(s_ck, b + 1)
                if b:
                    pool.wait_ge(s_num, b)
                den = rt[:, 5, :]
                seen_h = spread(seen[:, :].rearrange("p (n o) -> p n o", o=1), 2, H)
                link(pool.tensor_tensor(den.rearrange("p (i h) -> p i h", i=TB), ck[:, b % 2, :, :],
                                        seen_h, ALU.mult))
                pool.tensor_scalar(den, den, EPS, None, ALU.add).then_inc(s_dpre, 1)

            def scaled_q_terms(b):
                pool.wait_ge(s_qrem, b + 1)
                if b:
                    pool.wait_ge(s_qps, STACK_DMAS * b)
                pool.tensor_copy(QP3[:, 1, :], QREM).then_inc(s_qmid, 1)
                pool.wait_ge(s_qmid, b + 1)
                pool.tensor_tensor(QP3[:, 2, :], QREM, QP3[:, 1, :], ALU.subtract).then_inc(s_qlo, 1)

            def normalise(b):
                aof = AO.rearrange("p i h c -> p (i h) c")
                numf = NUM.rearrange("p i h c -> p (i h) c")
                pool.wait_ge(s_vp, b + 1)
                pool.wait_ge(s_ao, HP * (b + 1))
                link(pool.tensor_tensor(numf, numf, aof[:, :, 0:HD], ALU.add))
                pool.wait_ge(s_drec, b + 1)
                pool.tensor_tensor(numf, numf, spread(rt[:, 5, :].rearrange("p (n o) -> p n o", o=1),
                                                      2, HD), ALU.mult).then_inc(s_num, 1)

            for s in range(END_STEP):
                for b in range(NB):
                    at = s - b * HP
                    if at == A_AT:
                        agg_sums(b)
                    if at == R_AT:
                        scale_q(b)
                    if at == Q_AT:
                        scaled_q_terms(b)
                    if at == V_AT:
                        key_counts(b)
                    if at == N_AT:
                        normalise(b)
            scatter(1)
            gather(1)

        @block.scalar
        def _(act):
            def tables(number):
                act.add_instruction(mybir.InstLoadActFuncSet(
                    name=nc.get_next_instruction_name(), act_func_set_id=number,
                    engine=mybir.EngineType.Activation, ins=[], outs=[]))

            def layer_norm(k, xnt):
                act.wait_ge(s_var, k + 1)
                act.activation(lnt[:, 1, :], lnt[:, 0, :], ACT.Sqrt).then_inc(s_std, 1)
                for g in range(NB):
                    act.wait_ge(s_tp, NB * k + g + 1)
                    act.activation(xnt[:, g * SEQ:(g + 1) * SEQ], PS[:, g % 2, :], ACT.Copy)\
                        .then_inc(s_xnt, 1)

            def gelu(r, s, k):
                act.wait_ge(s_up, s + (r * NS + 1))
                for c in range(FC):
                    if c == 0 and (not isinstance(s, int) or s >= 2):
                        act.wait_ge(s_dn, s + (r * NS - 1))
                    last = act.activation(HT[:, k % 2, c * P:(c + 1) * P],
                                          PS[:, k % 2, c * P:(c + 1) * P], ACT.Gelu,
                                          bias=W1[:, k, F + c:F + c + 1])
                last.then_inc(s_h, 1)

            def ffn(r):
                layer_norm(2 * r, XNT1)
                act.wait_ge(s_sh, r + 1)
                act.activation(ex, sh, ACT.Exp).then_inc(s_ex, 1)
                for k in range(RING):
                    gelu(r, k, k)
                with act.Fori(1, NS // RING) as g:
                    for k in range(RING):
                        gelu(r, g * RING + k, k)
                for s in range(NS // RING * RING, NS):
                    gelu(r, s, s % RING)

            ffn(0)
            layer_norm(1, XNT2)

            def first_term(m):
                u, c = m // 2, m % 2
                act.wait_ge(s_pj, m + 1)
                if u == 5:
                    act.wait_ge(s_stk[0], STACK_DMAS)
                act.activation(SP3[u][:, 0, c * SEQ:(c + 1) * SEQ], PS[:, c, :], ACT.Copy)\
                    .then_inc(s_hi, 1)

            def second_term(m):
                u, c = m // 2, m % 2
                act.wait_ge(s_rem, m + 1)
                act.activation(SP3[u][:, 1, c * SEQ:(c + 1) * SEQ], REM[:, c, :], ACT.Copy)\
                    .then_inc(s_mid, 1)

            def terms(m0, m1):
                for m in range(m0, m1 + 1):
                    if m < m1:
                        first_term(m)
                    if m > m0:
                        second_term(m - 1)

            def q_rows(t):
                act.wait_ge(s_qv, t + 1)
                act.activation(QT[:, 2 * t:2 * t + 2, :],
                               PS[:, 2 + t % 2, :].rearrange("p (n c) -> p n c", n=2)[:, :, 0:P],
                               ACT.Copy).then_inc(s_qc, 1)

            terms(0, 6)
            for t in range(NT // 2):
                q_rows(t)
            terms(6, 12)

            def first_pass(s, tiles):
                for i in tiles:
                    n = (i + 1) * P
                    act.wait_ge(s_cl, 4 * s + (i + 1))
                    for par in range(2):
                        act.activation(CL[i][:, par, 0:n], CL[i][:, par, 0:n], ACT.Exp,
                                       scale=SCALE,
                                       accum_out=aggf[:, ds(s + (2 * i + par) * STEPS, 1)])\
                            .then_inc(s_e, 1)

            def second_pass(v):
                act.wait_ge(s_abs, 6 * v + 6)
                act.activation(WB[:, ds(v & 1, 1), :], WB[:, ds(v & 1, 1), :], ACT.Ln,
                               bias=1.0, scale=1.0).then_inc(s_ln, 1)

            def av_out(v):
                act.wait_ge(s_av, len(WEIGH_TILES) * v)
                act.activation(AOT, PS[:, 6, :], ACT.Copy).then_inc(s_aot, 1)

            tables(EXP_AND_LN)
            for s0, s1 in stretches((T_AT,)):
                with steps(act, s0, s1) as base:
                    for odd in range(2):
                        s = base + odd
                        if odd and LAG + 2 <= s0 < LAST_STEP:
                            av_out(s - LAG - 1)
                        if s0 < STEPS:
                            first_pass(s, range(TB))
                        if LAG <= s0 < STEPS + LAG:
                            second_pass(s - LAG)
                        for b in range(NB):
                            if s1 - s0 == 2 and s == b * HP + T_AT:
                                act.wait_ge(s_ot, b + 1)
                                act.wait_ge(s_qlo, min(b + 2, NB))
                                act.activation(OT, PS[:, 7, :], ACT.Copy).then_inc(s_otc, 1)
            ffn(1)

        @block.vector
        def _(dve):
            done = [0]

            def mark(ins, times=1):
                done[0] += times
                ins.then_inc(s_dve, 1)

            def settle():
                dve.wait_ge(s_dve, done[0])

            def link(ins):
                mark(ins)
                settle()

            def moments(b):
                for n in range(b * TB, (b + 1) * TB):
                    mark(dve.bn_stats(stats[:, n, :], X[:, n, :]))
                settle()
                for n in range(b * TB, (b + 1) * TB):
                    mark(dve.bn_aggr(mv[:, n, :], stats[:, n, :]))

            def layer_norm(k, xn):
                settle()
                dve.tensor_scalar(lnt[:, 0, :], mv[:, :, 1], LN_EPS, None, ALU.add).then_inc(s_var, 1)
                dve.wait_ge(s_std, k + 1)
                link(dve.reciprocal(lnt[:, 2, :], lnt[:, 1, :]))
                link(dve.tensor_tensor(lnt[:, 3, :], lnt[:, 2, :], lnt[:, 2, :], ALU.mult))
                link(dve.tensor_tensor(lnt[:, 3, :], lnt[:, 3, :], lnt[:, 0, :], ALU.mult))
                link(dve.tensor_scalar(lnt[:, 3, :], lnt[:, 3, :], -0.5, 1.5, ALU.mult, ALU.add))
                link(dve.tensor_tensor(lnt[:, 2, :], lnt[:, 2, :], lnt[:, 3, :], ALU.mult))
                for n in range(NT):
                    dve.tensor_scalar(xn[:, n, :], X[:, n, :], mv[:, n, 0:1], lnt[:, 2, n:n + 1],
                                      ALU.subtract, ALU.mult).then_inc(s_xn, 1)

            def over_n(a, k=NT):
                return spread(a.rearrange("p (o e) -> p o e", o=1), 1, k)

            def over_e(a, k=E):
                return spread(a.rearrange("p (n o) -> p n o", o=1), 2, k)

            def route(r):
                dve.wait_ge(s_sc, r + 1)
                sc = PS[:, 2, 0:NT * E].rearrange("p (n e) -> p n e", n=NT)
                link(dve.memset(oh[:, NT, :], 0.0))
                link(dve.reduce_max(mx, sc, axis=AX))
                dve.tensor_tensor(sh, sc, over_e(mx), ALU.subtract).then_inc(s_sh, 1)
                dve.wait_ge(s_sh, r + 1)
                dve.wait_ge(s_c, 7)
                link(dve.scalar_tensor_tensor(out=cand, in0=sh, scalar=0.0, in1=over_n(em8[:, :]),
                                              op0=ALU.is_ge, op1=ALU.mult))
                link(dve.tensor_reduce(cmin, cand, axis=AX, op=ALU.min))
                dve.tensor_tensor(oh[:, 0:NT, :], over_n(em8[:, :]), over_e(cmin), ALU.is_equal)\
                    .then_inc(s_oh, 1)
                dve.wait_ge(s_ex, r + 1)
                link(dve.reduce_sum(ssum, ex, axis=AX))
                link(dve.reciprocal(ssum, ssum))
                link(dve.tensor_scalar(coef[:, :], ssum, 0.5, None, ALU.mult))
                dve.wait_ge(s_rk, r + 1)
                link(dve.tensor_copy(cnt, PS[:, 3, NT * E:NT * E + E]))
                link(dve.tensor_tensor(ntc, over_e(cnt, NT), over_n(j128[:, :], E), ALU.is_gt))
                link(dve.reduce_sum(nt, ntc, axis=AX))
                link(dve.tensor_tensor(bsm, over_n(nt, E), lower8[:, :, :], ALU.mult))
                link(dve.reduce_sum(bst, bsm, axis=AX))
                link(dve.tensor_scalar(brow, bst, float(P), None, ALU.mult))
                link(dve.tensor_tensor(bend, bst, nt, ALU.add))
                link(dve.tensor_tensor(posm, PS[:, 3, 0:NT * E].rearrange("p (n e) -> p n e", n=NT),
                                       over_n(brow), ALU.add))
                link(dve.tensor_tensor(posm, posm, oh[:, 0:NT, :], ALU.mult))
                link(dve.reduce_sum(posf, posm, axis=AX))
                dve.tensor_copy(posi[:, :], posf).then_inc(s_pos, 1)
                link(dve.tensor_tensor(mapm, over_e(slot_no[:, :]), over_n(bend, NS), ALU.is_ge))
                link(dve.reduce_sum(mapf, mapm, axis=AX))
                link(dve.tensor_scalar(mapf, mapf, float(E - 1), None, ALU.min))
                dve.tensor_copy(emap[:, :], mapf).then_inc(s_pos, 1)

            def copy_xt(r, g, w):
                dve.wait_ge(s_px, g + (r * GROUPS + 1))
                dve.tensor_copy(XT[:, ds(g & 1, 1), 0:w], PS[:, ds((g & 1) + 4, 1), 0:w])\
                    .then_inc(s_vx, 1)

            def slot_out(r, s):
                dve.wait_ge(s_dn, s + (r * NS + 1))
                dve.tensor_copy(YO[:, ds(s, 1), :], PS[:, ds((s & 1) + 6, 1), 0:P]).then_inc(s_y, 1)

            def constants():
                dve.wait_ge(s_b, 16)
                link(dve.tensor_copy(BT[:, 0, :], BL))
                link(dve.tensor_tensor(BR, BL, BT[:, 0, :], ALU.subtract))
                link(dve.tensor_copy(BT[:, 1, :], BR))
                link(dve.tensor_tensor(BR, BR, BT[:, 1, :], ALU.subtract))
                dve.tensor_copy(BT[:, 2, :], BR).then_inc(s_bt, 1)
                dve.wait_ge(s_c, 7)
                link(dve.tensor_scalar(MB[:, :], MB[:, :], 1, None, ALU.logical_shift_right))

            def ffn(r):
                layer_norm(2 * r, XN1)
                if r == 0:
                    constants()
                route(r)

                copy_xt(r, 0, SEQ)
                with dve.Fori(0, GROUPS - 2) as g:
                    copy_xt(r, g + 1, SEQ)
                    for k in range(4):
                        slot_out(r, g * 4 + k)
                copy_xt(r, GROUPS - 1, (NS - 4 * (GROUPS - 1)) * P)
                for s in range(4 * (GROUPS - 2), NS):
                    slot_out(r, s)
                for b in range(NB):
                    dve.wait_ge(s_yg[b], 16 * TB * (r + 1))
                    for n in range(b * TB, (b + 1) * TB):
                        dve.scalar_tensor_tensor(out=X[:, n, :], in0=YG[:, n, :],
                                                 scalar=coef[:, n:n + 1], in1=X[:, n, :],
                                                 op0=ALU.mult, op1=ALU.add).then_inc(s_xr, 1)
                    if r == 0:
                        dve.wait_ge(s_xr, TB * (b + 1))
                        moments(b)

            for b in range(NB):
                dve.wait_ge(s_x[b], 16)
                moments(b)
            ffn(0)
            layer_norm(1, XN2)

            def remainder(m):
                u, c = m // 2, m % 2
                dve.wait_ge(s_hi, m + 1)
                if m >= 2:
                    dve.wait_ge(s_lo, m - 1)
                dve.tensor_tensor(REM[:, c, :], PS[:, c, :], SP3[u][:, 0, c * SEQ:(c + 1) * SEQ],
                                  ALU.subtract).then_inc(s_rem, 1)

            def v_rows(t):
                dve.wait_ge(s_qc, t + 1)
                for k in range(2):
                    dve.tensor_copy(V[:, 2 * t + k, :, 0:HD],
                                    PS[:, 2 + t % 2, k * 2 * P + P:(k + 1) * 2 * P].rearrange(
                                        "p (h c) -> p h c", h=H)).then_inc(s_vc, 1)

            for m in range(6):
                remainder(m)
            for t in range(NT // 2):
                v_rows(t)
            for m in range(6, 12):
                remainder(m)

            def clip_scores(s, i, first):
                n = (i + 1) * P
                dve.wait_ge(s_pa, 4 * s + (i + 1))
                if not first:
                    dve.wait_ge(s_e, 8 * s + (2 * i - 6))
                bank = 2 * (i % 2)
                dve.scalar_tensor_tensor(
                    out=CL[i][:, :, 0:n], in0=PS[:, bank:bank + 2, 0:n], scalar=-CLIP,
                    in1=spread(MA[:, SEQ - n:SEQ].rearrange("p (o n) -> p o n", o=1), 1, 2),
                    op0=ALU.max, op1=ALU.min).then_inc(s_cl, 1)

            def abs_scores(v, k, first):
                par, g = k // 3, k % 3
                n, at = SEG_N[g], par * HEAD_W + 512 * g
                dve.wait_ge(s_pb, 6 * v + (k + 1))
                if k < 2 and not first:
                    dve.wait_ge(s_av, 3 * v - (5 if k == 0 else 3))
                dve.tensor_tensor(
                    WB[:, ds(v & 1, 1), at:at + n].bitcast(i32), PS[:, 4 + k % 2:5 + k % 2, 0:n].bitcast(i32),
                    MB[:, SEG_MASK[g]:SEG_MASK[g] + n].rearrange("p (o n) -> p o n", o=1),
                    ALU.bitwise_and).then_inc(s_abs, 1)

            def heads_out(v):
                dve.wait_ge(s_aotp, (v >> 1) + 1)
                w = 2 * (HD + 1)
                for par in range(2):
                    at = ((v >> 1) & 3) * w + par * HP * (HD + 1)
                    dve.tensor_copy(
                        AO.rearrange("p i h c -> p i (h c)")[:, :, ds(at, w)],
                        PS[:, AO_BANK, AO_COL:AO_COL + TB * 2 * w].rearrange("p (i r) -> p i r", i=TB)
                        [:, :, par * w:(par + 1) * w]).then_inc(s_ao, 1)

            def v_prefix(b):
                dve.wait_ge(s_cv, b + 1)
                dve.wait_ge(s_ck, b + 1)
                if b:
                    dve.wait_ge(s_ot, b)
                dve.tensor_tensor(NUM.rearrange("p i h c -> p (i h) c"),
                                  PS[:, 7, :].rearrange("p (h c) -> p h c", c=HD),
                                  over_e(ckf(b), HD), ALU.mult).then_inc(s_vp, 1)

            def scaled_q_terms(b):
                dve.wait_ge(s_qt, b + 1)
                if b:
                    dve.wait_ge(s_qps, STACK_DMAS * b)
                dve.tensor_copy(QP3[:, 0, :], PS[:, 7, :]).then_inc(s_qhi, 1)
                dve.wait_ge(s_qhi, b + 1)
                dve.tensor_tensor(QREM, PS[:, 7, :], QP3[:, 0, :], ALU.subtract).then_inc(s_qrem, 1)

            def after(s):
                for b in range(NB):
                    at = s - b * HP
                    if at == R_AT:
                        dve.wait_ge(s_apre, b + 1)
                        dve.reciprocal(rt[:, 0:2, :], rt[:, 0:2, :]).then_inc(s_arec, 1)
                    if at == Q_AT:
                        scaled_q_terms(b)
                    if at == V_AT:
                        v_prefix(b)
                    if at == N_AT:
                        dve.wait_ge(s_dpre, b + 1)
                        dve.wait_ge(s_ao, HP * (b + 1))
                        den = rt[:, 5, :]
                        link(dve.tensor_tensor(den, den, AO.rearrange("p i h c -> p (i h) c")[:, :, HD],
                                               ALU.add))
                        dve.reciprocal(den, den).then_inc(s_drec, 1)
                    if at == X_AT:
                        dve.wait_ge(s_pr, b + 1)
                        xb = X[:, b * TB:(b + 1) * TB, :]
                        dve.tensor_tensor(xb, PS[:, 7, :].rearrange("p (n d) -> p n d", n=TB), xb,
                                          ALU.add).then_inc(s_xr, 1)
                        dve.wait_ge(s_xr, NT + b + 1)
                        moments(b)

            dve.wait_ge(s_lo, 12)
            dve.wait_ge(s_stk[1], STACK_DMAS)
            for s0, s1 in stretches((R_AT, Q_AT, V_AT, N_AT, X_AT)):
                with steps(dve, s0, s1) as base:
                    for odd in range(2):
                        s, v = base + odd, base + (odd - LAG)
                        for k in range(6):
                            if s0 < STEPS and k < TB:
                                clip_scores(s, k, s0 == 0 and not odd)
                            if LAG <= s0 < STEPS + LAG:
                                abs_scores(v, k, s0 == LAG)
                            if k == AO_K and odd and LAG + 2 <= s0 < LAST_STEP:
                                heads_out(v - 3)
                        if s1 - s0 == 2:
                            after(s)
            ffn(1)

        @block.tensor
        def _(pe):
            def layer_norm(k, xn):
                for g in range(NB):
                    pe.wait_ge(s_xn, NT * k + TB * (g + 1))
                    if g >= 2:
                        pe.wait_ge(s_xnt, NB * k + g - 1)
                    for j in range(TB):
                        last = pe.transpose(PS[:, g % 2, j * P:(j + 1) * P], xn[:, g * TB + j, :],
                                            ident[:, :])
                    last.then_inc(s_tp, 1)
                    if k != 1 and g:
                        gate(k // 2, g - 1)
                if k != 1:
                    gate(k // 2, NB - 1)

            def gate(r, g):
                pe.wait_ge(s_xnt, 2 * NB * r + g + 1)
                for n in range(g * TB, (g + 1) * TB):
                    last = pe.matmul(PS[:, 2, n * E:(n + 1) * E], XNT1[:, n * P:(n + 1) * P], WG[:, :],
                                     start=True, stop=True)
                if g == NB - 1:
                    last.then_inc(s_sc, 1)

            def route(r):
                pe.wait_ge(s_oh, r + 1)
                pe.matmul(PS[:, 3, 0:(NT + 1) * E], utri[:, :], oh, start=True, stop=False)
                for n in range(NT):
                    last = pe.matmul(PS[:, 3, (n + 1) * E:(NT + 1) * E], onesb[:, :],
                                     spread(oh[:, n:n + 1, :], 1, NT - n), start=False, stop=n == NT - 1)
                last.then_inc(s_rk, 1)

            def slot_transposes(r, g):
                pe.wait_ge(s_xs[r][g], 16)
                if g >= 2:
                    pe.wait_ge(s_vx, r * GROUPS + g - 1)
                for s in range(4 * g, min(4 * g + 4, NS)):
                    last = pe.transpose(PS[:, 4 + g % 2, (s % 4) * P:(s % 4 + 1) * P], XS[:, s, :],
                                        ident[:, :])
                last.then_inc(s_px, 1)

            def up(r, s):
                if s % 4 == 0:
                    pe.wait_ge(s_vx, r * GROUPS + s // 4 + 1)
                if s >= 2:
                    pe.wait_ge(s_h, r * NS + s - 1)
                pe.wait_ge(s_w1[s % RING], 16 * (r * ring_uses(s % RING) + s // RING + 1))
                for c in range(FC):
                    last = pe.matmul(PS[:, s % 2, c * P:(c + 1) * P],
                                     W1[:, s % RING, c * P:(c + 1) * P],
                                     XT[:, s // 4 % 2, (s % 4) * P:(s % 4 + 1) * P],
                                     start=True, stop=True)
                last.then_inc(s_up, 1)

            def down(r, s):
                e = pe.value_load(emap[0:1, s:s + 1], min_val=0, max_val=E - 1)
                pe.wait_ge(s_h, r * NS + s + 1)
                if s >= 2:
                    pe.wait_ge(s_y, r * NS + s - 1)
                pe.matmul(PS[:, 6 + s % 2, 0:P], onesb[0:TERMS, :], BS[:, ds(e * P, P)],
                          start=True, stop=False)
                for c in range(FC):
                    last = pe.matmul(PS[:, 6 + s % 2, 0:P], HT[:, s % 2, c * P:(c + 1) * P],
                                     W2[:, ds(e * F + c * P, P)], start=False, stop=c == FC - 1)
                last.then_inc(s_dn, 1)

            def ring_uses(k):
                return len(range(k, NS, RING))

            def ffn(r):
                layer_norm(2 * r, XN1)
                route(r)
                pe.wait_ge(s_pos, 2 * r + 2)
                pe.wait_ge(s_bs, 16 * (r + 1))
                slot_transposes(r, 0)
                for s in range(NS + 1):
                    if s < NS:
                        up(r, s)
                        if s % 4 == 1 and s // 4 + 1 < GROUPS:
                            slot_transposes(r, s // 4 + 1)
                    if s == 1:
                        pe.wait_ge(s_w2, 16 * (r + 1))
                    if s >= 1:
                        down(r, s - 1)

            pe.wait_ge(s_c, 7)
            pe.wait_ge(s_wg, 16)
            ffn(0)
            layer_norm(1, XN2)
            pe.wait_ge(s_wa, 16)
            pe.wait_ge(s_xnt, 2 * NB)

            def project(m):
                which, w = UNITS[m // 2]
                if m >= 2:
                    pe.wait_ge(s_hi, m - 1)
                    pe.wait_ge(s_rem, m - 1)
                at = w * 2 * SEQ + (m % 2) * SEQ
                pe.matmul(PS[:, m % 2, :], WA[:, WCOL[which], :], XNT2[:, at:at + SEQ],
                          start=True, stop=True).then_inc(s_pj, 1)

            def q_v_rows(t):
                if t >= 2:
                    pe.wait_ge(s_qc, t - 1)
                    pe.wait_ge(s_vc, 2 * (t - 1))
                for k in range(2):
                    n = 2 * t + k
                    last = pe.matmul(PS[:, 2 + t % 2, k * 2 * P:(k + 1) * 2 * P],
                                     XNT2[:, n * P:(n + 1) * P], WA[:, 0:2, :], start=True, stop=True)
                last.then_inc(s_qv, 1)

            for m in range(6):
                project(m)
            for t in range(NT // 2):
                q_v_rows(t)
            for m in range(6, 12):
                project(m)

            def scores_a(s, i):
                b, hp, n = s // HP, s % HP, (i + 1) * P
                a = 4 * s + i
                if a >= 2:
                    pe.wait_ge(s_cl, a - 1)
                for par in range(2):
                    rows = slice(64 * par, 64 * par + KROWS)
                    last = pe.matmul(PS[:, 2 * (i % 2) + par, 0:n],
                                     QS[rows, hp, (b * TB + i) * P:(b * TB + i + 1) * P],
                                     YS[rows, hp, b * SEQ:b * SEQ + n], start=True, stop=True)
                last.then_inc(s_pa, 1)

            def scores_b(v, k):
                b, hp, par, g = v // HP, v % HP, k // 3, k % 3
                c = 6 * v + k
                if c >= 2:
                    pe.wait_ge(s_abs, c - 1)
                if k == 1 and v % 2 == 0 and v >= 4:
                    pe.wait_ge(s_ao, v - 2)
                rows = slice(64 * par, 64 * par + KROWS)
                at = 0
                for j in SEG_J[g]:
                    n = SEQ - j * P
                    last = pe.matmul(PS[:, 4 + k % 2, at:at + n],
                                     KS[rows, hp, (b * TB + j) * P:(b * TB + j + 1) * P],
                                     QPS[rows, b % 2, hp, j * P:SEQ], start=True, stop=True)
                    at += n
                last.then_inc(s_pb, 1)

            def weigh(v, tiles):
                b, hp = v // HP, v % HP
                if tiles[0] == 0:
                    pe.wait_ge(s_ln, v + 1)
                    if v >= 2:
                        pe.wait_ge(s_aot, v // 2)
                for j in tiles:
                    for par in range(2):
                        quad = QUAD * (2 * par + v % 2)
                        at = par * HEAD_W + J_OFF[j]
                        head = ((b * TB + j) * H + par * HP + hp) * (HD + 1)
                        last = pe.matmul(PS[quad:quad + QUAD, 6, j * P:SEQ], VF[:, head:head + QUAD],
                                         WB[:, v % 2, at:at + SEQ - j * P],
                                         start=j == 0, stop=j == TB - 1)
                last.then_inc(s_av, 1)

            def weighed_t(v):
                pe.wait_ge(s_aot, v // 2 + 1)
                pe.wait_ge(s_abs, min(6 * (v + 3) + AO_K - 1, 6 * STEPS))
                if v >= 2:
                    pe.wait_ge(s_ao, v // 2 * 2)
                used = ident[:, :].rearrange("p (q r) -> p q r", r=QUAD)[:, :, 0:HD + 1]
                for i in range(TB):
                    at = AO_COL + i * 4 * (HD + 1)
                    last = pe.matmul(PS[:, AO_BANK, at:at + 4 * (HD + 1)], AOT[:, i * P:(i + 1) * P],
                                     used, start=True, stop=True)
                last.then_inc(s_aotp, 1)

            def v_prefix(b, shift):
                if shift == 0:
                    if b + 1 < NB:
                        pe.wait_ge(s_qrem, b + 2)
                    if b:
                        pe.wait_ge(s_xr, NT + b)
                last = pe.matmul(PS[:, 7, shift * P:SEQ], (ones if shift else tri)[:, :],
                                 V[:, b * TB:(b + 1) * TB - shift, :, 0:HD], start=shift == 0,
                                 stop=shift == TB - 1)
                if shift == TB - 1:
                    last.then_inc(s_cv, 1)

            def after(s):
                for b in range(NB):
                    at = s - b * HP
                    if at == Q_AT:
                        pe.wait_ge(s_qsc, TB * (b + 1))
                        if b >= 2:
                            pe.wait_ge(s_xr, NT + b - 1)
                        for i in range(TB):
                            last = pe.transpose(PS[:, 7, i * P:(i + 1) * P], QT[:, b * TB + i, :],
                                                ident[:, :])
                        last.then_inc(s_qt, 1)
                    if at == T_AT:
                        pe.wait_ge(s_num, b + 1)
                        for i in range(TB):
                            last = pe.transpose(PS[:, 7, i * P:(i + 1) * P],
                                                NUM[:, i, :, :].rearrange("p h c -> p (h c)"), ident[:, :])
                        last.then_inc(s_ot, 1)
                    if at == P_AT:
                        pe.wait_ge(s_otc, b + 1)
                        for i in range(TB):
                            last = pe.matmul(PS[:, 7, i * P:(i + 1) * P], OT[:, i * P:(i + 1) * P],
                                             WA[:, 4, :], start=True, stop=True)
                        last.then_inc(s_pr, 1)

            pe.wait_ge(s_hi, 12)
            pe.wait_ge(s_rem, 12)
            pe.wait_ge(s_qc, NT // 2)
            pe.wait_ge(s_vc, NT)
            for s in range(END_STEP):
                v = s - LAG
                for u, (which, w) in enumerate(UNITS):
                    if (v if which == 2 else s) == w * 2 * HP:
                        pe.wait_ge(s_stk[u], STACK_DMAS)
                if 0 <= v < STEPS and v % HP == 0:
                    pe.wait_ge(s_qps, STACK_DMAS * (v // HP + 1))
                for k in range(6):
                    if s < STEPS and k < TB:
                        scores_a(s, k)
                    if k == AO_K and v % 2 and 3 <= v <= STEPS + 1:
                        weighed_t(v - 3)
                    if 0 <= v < STEPS:
                        scores_b(v, k)
                    if k < TB and s % HP == C_AT % HP and 0 <= s - C_AT < STEPS:
                        v_prefix((s - C_AT) // HP, k)
                    if 1 <= v <= STEPS and k >= 3:
                        weigh(v - 1, WEIGH_TILES[k - 3])
                after(s)
            ffn(1)


def kernel(L0_attn_x, L0_attn_w_qkv, L0_attn_w_ky, L0_attn_w_proj, L0_ffn_Wg, L0_ffn_W1, L0_ffn_b1,
           L0_ffn_W2, L0_ffn_b2):
    import concourse.bacc as bacc
    from concourse.bass_utils import run_bass_kernel_spmd

    def c(a):
        return np.ascontiguousarray(a)

    wq, wk, wv = np.split(np.asarray(L0_attn_w_qkv), 3, axis=0)

    def by_channel(w):
        return np.transpose(np.asarray(w).reshape(HP, 2, HD, P), (1, 2, 0, 3)).reshape(P, P).T

    def by_head(w):
        return np.transpose(np.asarray(w).reshape(HP, 2, HD, P), (1, 0, 2, 3)).reshape(P, P).T

    proj = np.transpose(np.asarray(L0_attn_w_proj).reshape(P, HP, 2, HD), (2, 1, 3, 0)).reshape(P, P)
    wattn = np.stack([by_channel(wq), by_head(wv), by_channel(L0_attn_w_ky), by_channel(wk), proj], 1)
    arrays = {
        "x": c(np.asarray(L0_attn_x).reshape(NT * P, P)),
        "wattn": c(wattn),
        "wg": c(np.asarray(L0_ffn_Wg).T),
        "w1": c(np.concatenate([np.transpose(np.asarray(L0_ffn_W1), (0, 2, 1)),
                                np.transpose(np.asarray(L0_ffn_b1).reshape(E, FC, P), (0, 2, 1))], 2)),
        "w2": c(np.transpose(np.asarray(L0_ffn_W2).reshape(E, P, FC, P), (3, 0, 2, 1)).reshape(P, E * F)),
        "b2": c(L0_ffn_b2),
    }
    nc = bacc.Bacc("TRN2", target_bir_lowering=False, num_devices=1)
    args = [nc.dram_tensor(n, a.shape, mybir.dt.from_np(a.dtype), kind="ExternalInput").ap()
            for n, a in arrays.items()]
    out = nc.dram_tensor("out", (NT * P, P), mybir.dt.float32, kind="ExternalOutput").ap()
    build(nc, *args, out)
    r = run_bass_kernel_spmd(nc, [arrays], core_ids=[0])
    return r.results[0]["out"].reshape(NB, SEQ, P)
```

```python
import numpy as np
import concourse.bass as bass
from concourse import mybir
from contextlib import ExitStack

P = 128
NT = 16
NB, TB = 4, 4
SEQ = TB * P
E, F = 8, 512
FC = F // P
W1_W = F + FC
ROW = P + 1
RING = 4
E_ROWS = NT * P + P
SP_SLOTS, ACT_SLOTS = (0, 1, 4, 5), (2, 3, 6, 7)
NS = NT + E - 1
H, HD = 16, 8
HP = H // 2
TERMS = 3
Q_TERMS = (0, 0, 1, 1, 0, 2)
K_TERMS = (0, 1, 0, 1, 2, 0)
KROWS = HD * len(Q_TERMS)
EXP_AND_LN = 6
EPS = 1e-6
LN_EPS = 1e-5
SCALE = float(1.0 / np.sqrt(HD))
CLIP = 15.0 / SCALE
MASKED = -3.0e4
STEPS = NB * HP
LAG = HP + 4
SEG_J = ((0,), (3, 1), (2,))
SEG_N = (512, 512, 256)
SEG_MASK = (128, 0, 128)
PIECES = {3: (0,), 4: (1,), 5: (2,), 6: (3,)}
TAIL_PIECES = {3: (0,), 4: (1,), 5: (2, 3)}
QUAD = 32
PJ_BANK = (0, 4)
QV_BANK = (2, 6)
WEIGH_TILES = (0, 1, 3, 2)
AO_K, AO_COL = 4, 256
J_OFF = {0: 0, 3: 512, 1: 640, 2: 1024}
HEAD_W = 1280
STACK_DMAS = 16 * 2 * len(Q_TERMS)
GROUPS = -(-NS // 4)
A_AT = HP - 1
R_AT = A_AT + 1
Q_AT = R_AT + 1
C_AT = LAG + HP - 1
V_AT = C_AT + 1
N_AT = LAG + HP + 1
T_AT = N_AT + 1
P_AT = T_AT + 1
X_AT = P_AT + 1
TAIL = STEPS - LAG
TAIL_BANKS = (0, 1, 2, 4, 0, 5)
END_STEP = (NB - 1) * HP + X_AT + 2


LN_PARTS = ((0, 0, 2), (0, 2, 4), (1, 0, 2), (1, 2, 4), (2, 0, 3), (2, 3, 4))
LN_EARLY = (NB - 1) * HP + LAG - 1 + HP
TURN_EARLY = (NB - 1) * HP + N_AT + 1
ROUTE_TILES = (((0, 8), (8, 16)), ((0, 4), (4, 12), (12, 16)))
SCORE_BANKS, RANK_BANKS = (2, 3, 6), (4, 5, 7)


def part_no(r, i):
    return r * len(ROUTE_TILES[0]) + i + 1


def late(b):
    return int((b + 1) * HP > TAIL)


def leaving(v):
    e = v - 3 if v < TAIL + 3 else v - 4
    return e if e % 2 == 0 and 0 <= e < STEPS and (e < TAIL) == (v < TAIL + 3) else None


def left(v):
    return sum(leaving(u) is not None for u in range(v))


def build(nc, x_in, wattn_in, wg_in, w1_in, w2_in, b2_in, out):
    f32, bf16, u32, i32 = mybir.dt.float32, mybir.dt.bfloat16, mybir.dt.uint32, mybir.dt.int32
    ALU, ACT, AX = mybir.AluOpType, mybir.ActivationFunctionType, mybir.AxisListType.X
    ds = bass.ds
    ctx = ExitStack()
    with ctx:
        def sb(name, shape, dt=f32):
            return ctx.enter_context(nc.sbuf_tensor(name, shape, dt))

        def sem(name):
            return ctx.enter_context(nc.semaphore(name))

        X = sb("X", [P, NT, P])
        R1 = sb("R1", [P, 8192])
        W1 = R1[:, 0:RING * W1_W].rearrange("p (r n) -> p r n", r=RING)
        W2 = R1[:, RING * W1_W:RING * W1_W + E * F]
        XN2 = R1[:, 0:2048].rearrange("p (n d) -> p n d", n=NT)
        XNT2 = R1[:, 2048:4096]
        REM = R1[:, 4096:5120].rearrange("p (r n) -> p r n", r=2)
        WB = R1[:, 0:5120].rearrange("p (r n) -> p r n", r=2)
        QP3 = R1[:, 5120:5888].bitcast(bf16).rearrange("p (t n) -> p t n", t=TERMS)
        AOT = R1[:, 5888:6400]
        AO = R1[:, 6400:6976].rearrange("p (i h c) -> p i h c", i=TB, h=H)
        NUM = R1[:, 6976:7488].rearrange("p (i h c) -> p i h c", i=TB, h=H)
        OT = R1[:, 7488:8000]
        QREM = OT
        stats = R1[:, 8000:8096].rearrange("p (n s) -> p n s", n=NT)
        mv = R1[:, 8096:8128].rearrange("p (n s) -> p n s", n=NT)
        lnt = R1[:, 8128:8192].rearrange("p (k n) -> p k n", k=4)
        R2 = sb("R2", [P, 4608])
        R2W = R2[:, :].rearrange("p (r n) -> p r n", r=3)[:, 0:3:2, 0:HEAD_W]
        R2B = R2[:, :].bitcast(bf16).rearrange("p (r t n) -> p r t n", r=3, t=TERMS)
        R3 = sb("R3", [P, 24576])
        stacks = R3[:, :].bitcast(bf16).rearrange("p (s q n) -> p s q n", s=3, q=HP)
        QS, YS, KS = stacks[:, 0], stacks[:, 1], stacks[:, 2]
        XS_ROWS = R3[:, 0:NS * ROW].rearrange("p (s d) -> p s d", s=NS)
        XS = XS_ROWS[:, :, 0:P]
        YO = R3[:, 2968:2968 + NS * P].rearrange("p (s d) -> p s d", s=NS)
        XN1_ROWS = R3[:, 5912:5912 + NT * ROW].rearrange("p (n d) -> p n d", n=NT)
        XN1 = XN1_ROWS[:, :, 0:P]
        XNT1 = R3[:, 10496:12544]
        Z = R3[:, 15808:15808 + ROW]
        YG = R3[:, 20480:22528].rearrange("p (n d) -> p n d", n=NT)
        HT = R3[:, 8960:9984].rearrange("p (r n) -> p r n", r=2)
        BS = R3[0:TERMS, 9984:10496].bitcast(bf16)
        BL = R3[0:E, 12544:12672]
        BR = R3[0:E, 12672:12800]
        BT = R3[0:E, 13824:14016].bitcast(bf16).rearrange("p (t n) -> p t n", t=TERMS)
        XT = R3[:, 14784:15808].rearrange("p (r n) -> p r n", r=2)
        T3 = R3[:, 16384:24576]
        sh = T3[:, 0:128].rearrange("p (n e) -> p n e", n=NT)
        ex = T3[:, 128:256].rearrange("p (n e) -> p n e", n=NT)
        cand = T3[:, 256:384].rearrange("p (n e) -> p n e", n=NT)
        posm = T3[:, 384:512].rearrange("p (n e) -> p n e", n=NT)
        ntc = T3[:, 512:640].rearrange("p (e j) -> p e j", e=E)
        bsm = T3[:, 640:704].rearrange("p (e j) -> p e j", e=E)
        mapm = T3[:, 704:704 + NS * E].rearrange("p (s e) -> p s e", s=NS)
        rt = sb("rt", [P, 6, TB * H])
        mx, cmin, ssum, posf = (T3[:, 896 + 16 * k:912 + 16 * k] for k in range(4))
        cnt, nt, bst, bend = (T3[:, 960 + 8 * k:968 + 8 * k] for k in range(4))
        mapf = T3[:, 1000:1000 + NS]
        oh = T3[:, 1024:1092].bitcast(bf16).rearrange("p (n e) -> p n e", n=NT + 1)
        posx = T3[:, 1100:1116].bitcast(u32)
        zrow = T3[:, 1120:1128].bitcast(u32)
        srow = T3[:, 1130:1130 + NS].bitcast(u32)
        ends, hole = T3[:, 1160:1168], T3[:, 1168:1176]
        holes, rowf, used = (T3[:, 1180 + 30 * k:1180 + 30 * k + NS] for k in range(3))
        holem = T3[:, 1270:1270 + NS * E].rearrange("p (s e) -> p s e", s=NS)
        QT = sb("QT", [P, NT, P])
        VF = sb("V", [P, NT * H * (HD + 1) + QUAD])
        V = VF[:, 0:NT * H * (HD + 1)].rearrange("p (n h c) -> p n h c", n=NT, h=H)
        QPS = sb("QPS", [P, 2, HP, SEQ], bf16)
        QB = QPS[:, :, :, :].rearrange("p r q n -> p (r q n)")[:, 0:2 * TERMS * 2 * SEQ]\
            .rearrange("p (r t n) -> p r t n", r=2, t=TERMS)
        SP3 = (R2B[:, 0], R2B[:, 1], R2B[:, 2], QB[:, 0], QB[:, 1], R2B[:, 0])
        CL3 = sb("CL3", [P, 2, SEQ])
        CL = [R2[:, 1536 + a:1536 + a + 2 * n].rearrange("p (r n) -> p r n", r=2)
              for a, n in ((0, P), (2 * P, 2 * P), (6 * P, 3 * P))] + [CL3]
        WA = sb("WA", [P, 5, P])
        WG = sb("WG", [P, E])
        ident = sb("ident", [P, P])
        tri = sb("tri", [P, P])
        ones = sb("ones", [P, P])
        MA = sb("MA", [P, SEQ])
        MB = sb("MB", [P, 5 * P], i32)
        utri = sb("utri", [P, P], bf16)
        onesb = sb("onesb", [P, P], bf16)
        em8 = sb("em8", [P, E])
        erow = sb("erow", [P, E])
        j128 = sb("j128", [P, NT])
        lower8 = sb("lower8", [P, E, E])
        slot_no = sb("slot_no", [P, NS])
        seen = sb("seen", [P, TB])
        agg = sb("agg", [P, TB, 2, STEPS])
        ck = sb("ck", [P, 2, TB, H])
        coef = sb("coef", [P, NT])
        spare = sb("spare", [P, NS])
        dest = sb("dest", [P, NS], u32)
        emap = sb("emap", [P, NS], u32)
        PS = ctx.enter_context(nc.psum_tensor("PS", [P, 8, 512], f32))
        xs_d = nc.dram_tensor("xs_d", (E * E_ROWS, ROW), f32, kind="Internal").ap()
        y_d = nc.dram_tensor("y_d", (NT * P + NS * P, P), f32, kind="Internal").ap()
        bs_d = nc.dram_tensor("bias_terms_d", (TERMS, E * P), bf16, kind="Internal").ap()

        s_x = [sem(f"x_{b}_loaded") for b in range(NB)]
        s_wg = sem("gate_weights_loaded")
        s_wa = sem("attn_weights_loaded")
        s_w1 = [sem(f"w1_ring_{k}_loaded") for k in range(RING)]
        s_w2 = sem("w2_loaded")
        s_b = sem("biases_loaded")
        s_bt = sem("bias_terms_ready")
        s_bd = sem("bias_terms_stored")
        s_bs = sem("bias_rows_loaded")
        s_z = sem("zero_tile_ready")
        s_zd = sem("padding_zeroed")
        s_row = sem("scratch_rows_ready")
        s_cnt = sem("expert_ends_ready")
        s_c0 = sem("const_fill")
        s_c = sem("consts_ready")
        s_dve = sem("dve_chain")
        s_var = sem("variance_ready")
        s_std = sem("std_ready")
        s_xn = sem("xn_ready")
        s_tp = sem("xnt_transposed")
        s_xnt = sem("xnt_copied")
        s_sc = sem("scores_ready")
        s_sh = sem("shifted_scores")
        s_ex = sem("exp_scores")
        s_oh = sem("onehot_ready")
        s_rk = sem("ranks_ready")
        s_pos = sem("slot_map_ready")
        s_sct = sem("rows_scattered")
        s_xs = [[sem(f"slots_{r}_{g}_loaded") for g in range(GROUPS)] for r in range(2)]
        s_px = sem("slot_transposed")
        s_vx = sem("slot_t_copied")
        s_up = sem("up_done")
        s_h = sem("gelu_done")
        s_dn = sem("down_done")
        s_y = sem("y_copied")
        s_dest = sem("destinations_ready")
        s_yd = sem("y_scattered_back")
        s_yg = [sem(f"y_{b}_loaded") for b in range(NB)]
        s_xr = sem("residual_ready")
        s_pj = sem("projection_done")
        s_hi = sem("first_term_ready")
        s_rem = sem("remainder_ready")
        s_lo = sem("terms_ready")
        s_mid = sem("second_term_ready")
        s_stk = [sem(f"stack_{i}_written") for i in range(6)]
        s_qv = sem("qv_done")
        s_qc = sem("q_copied")
        s_vc = sem("v_copied")
        s_pa = sem("ly_ready")
        s_cl = sem("clipped")
        s_e = sem("exp_summed")
        s_qsc = sem("q_scaled")
        s_qt = sem("scaled_q_transposed")
        s_qhi = sem("scaled_q_first_term")
        s_qrem = sem("scaled_q_remainder")
        s_qmid = sem("scaled_q_second_term")
        s_qlo = sem("scaled_q_terms_ready")
        s_qps = sem("scaled_q_stacked")
        s_pb = sem("l_ready")
        s_abs = sem("abs_done")
        s_ln = sem("ln_done")
        s_av = sem("av_done")
        s_aot = sem("av_out_of_psum")
        s_aotp = sem("av_transposed")
        s_ao = sem("av_copied")
        s_cv = sem("v_prefix_done")
        s_pool = sem("pool_chain")
        s_apre = sem("agg_sums_ready")
        s_arec = sem("agg_reciprocals_ready")
        s_dpre = sem("denominator_part_ready")
        s_drec = sem("denominator_reciprocal_ready")
        s_ck = sem("ck_ready")
        s_vp = sem("v_prefix_scaled")
        s_num = sem("attn_out_ready")
        s_ot = sem("attn_out_transposed")
        s_otc = sem("attn_out_t_copied")
        s_pr = sem("attn_projected")
        s_out = sem("output_stored")

        aggf = agg[:, :, :, :].rearrange("p i par s -> p (i par s)")
        UNITS = ((0, 0), (1, 0), (2, 0), (0, 1), (1, 1), (2, 1))
        WCOL = (0, 2, 3)

        def b_bank(k, alone):
            return TAIL_BANKS[k] if alone else 4 + k % 2

        def weights(v):
            ring = [wb.rearrange("p (r n) -> p r n", r=2) for wb in (WB[:, 0], WB[:, 1])] + [R2W]
            if v < TAIL:
                return ring[v % 3]
            return ([ring[(TAIL + k) % 3] for k in range(3)] + [None])[(v - TAIL) % 4]

        def head_weights(v, par):
            wb = weights(v)
            if wb is None:
                return R2[:, 1536:1536 + HEAD_W] if par == 0 else \
                    QT[:, :, :].rearrange("p n c -> p (n c)")[:, 0:HEAD_W]
            return wb[:, par]

        def av_bank(v):
            return 3 if v >= TAIL and v // 2 % 2 == TAIL // 2 % 2 else 6

        def stack_rows(par, t):
            return slice(64 * par + HD * t, 64 * par + HD * t + HD)

        def half(w):
            return slice(w * 2 * SEQ, (w + 1) * 2 * SEQ)

        def spread(a, axis, n):
            shape = list(a.shape)
            shape[axis] = n
            return a.broadcast_to(shape)

        def ckf(b):
            return ck[:, b % 2, :, :].rearrange("p i h -> p (i h)")

        block = ctx.enter_context(nc.Block())


        def rows_of(terms, term):
            return [t for t in range(len(terms)) if terms[t] == term]

        def load_x(engine, r, slots):
            for i in range(0, len(slots), 4):
                group = slots[i:i + 4]
                rows = [engine.value_load(srow[0:1, s:s + 1], min_val=0, max_val=E * E_ROWS - P)
                        for s in group]
                engine.wait_ge(s_sct, 16 * NT * (r + 1))
                engine.wait_ge(s_zd, 16 * E * (r + 1))
                for s, row in zip(group, rows):
                    engine.dma_start(XS_ROWS[:, s, :], xs_d[ds(row, P), :]).then_inc(s_xs[r][s // 4], 16)

        def pad(engine, r, experts):
            engine.wait_ge(s_z, 3 * (r + 1))
            engine.wait_ge(s_cnt, r + 1)
            for e in experts:
                row = engine.value_load(zrow[0:1, e:e + 1], min_val=0, max_val=E * E_ROWS - P)
                engine.dma_start(xs_d[ds(row, P), :], Z).then_inc(s_zd, 16)

        @block.sync
        def _(sp):
            for b in range(NB):
                sp.dma_start(X[:, b * TB:(b + 1) * TB, :],
                             x_in[b * SEQ:(b + 1) * SEQ, :].rearrange("(n p) d -> p n d", p=P))\
                    .then_inc(s_x[b], 16)
            sp.dma_start(WG[:, :], wg_in).then_inc(s_wg, 16)
            sp.dma_start(BL, b2_in).then_inc(s_b, 16)
            sp.dma_start(W2, w2_in).then_inc(s_w2, 16)
            sp.dma_start(WA[:, :, :], wattn_in).then_inc(s_wa, 16)

            def load_w1(r, s, k):
                e = sp.value_load(emap[0:1, ds(s, 1)], min_val=0, max_val=E - 1)
                sp.wait_ge(s_h, s + (r * NS - RING + 1))
                sp.dma_start(W1[:, k, :], w1_in[ds(e, 1), :, :].rearrange("o p n -> p (o n)"))\
                    .then_inc(s_w1[k], 16)

            def slots(r):
                pad(sp, r, range(0, E // 2))
                sp.wait_ge(s_pos, r + 1)
                load_x(sp, r, SP_SLOTS)
                if r == 0:
                    sp.wait_ge(s_bt, 1)
                    sp.dma_start(bs_d.rearrange("t (e n) -> e t n", e=E), BT).then_inc(s_bd, 16)
                    sp.wait_ge(s_bd, 16)
                    sp.dma_start(BS, bs_d).then_inc(s_bs, 16)
                with sp.Fori(0, NS // RING - 1) as g:
                    for k in range(RING):
                        load_w1(r, g * RING + (RING + k), k)
                done = (NS // RING - 1) * RING
                for k in range(NS % RING):
                    load_w1(r, done + RING + k, k)
                sp.wait_ge(s_yd, 16 * NS * (r + 1))
                for b in range(NB):
                    sp.dma_start(YG[:, b * TB:(b + 1) * TB, :],
                                 y_d[b * SEQ:(b + 1) * SEQ, :].rearrange("(n p) d -> p n d", p=P))\
                        .then_inc(s_yg[b], 16)

            slots(0)
            for u, (which, w) in enumerate(UNITS):
                if u == 2:
                    sp.wait_ge(s_xr, NT)
                dst = (QS, YS, KS)[which]
                for term, ready in enumerate((s_hi, s_mid, s_lo)):
                    sp.wait_ge(ready, 2 * (u + 1))
                    for t in rows_of(K_TERMS if which else Q_TERMS, term):
                        for par in range(2):
                            sp.dma_start(dst[stack_rows(par, t), :, half(w)],
                                         SP3[u][64 * par:64 * par + 64, term, :])\
                                .then_inc(s_stk[u], 16)
            sp.wait_ge(s_stk[3], STACK_DMAS)
            sp.wait_ge(s_stk[4], STACK_DMAS)
            for b in range(NB):
                if b >= 2:
                    sp.wait_ge(s_pb, 6 * HP * (b - 1))
                for term, ready in enumerate((s_qhi, s_qmid, s_qlo)):
                    sp.wait_ge(ready, b + 1)
                    for t in rows_of(Q_TERMS, term):
                        for par in range(2):
                            sp.dma_start(QPS[stack_rows(par, t), b % 2, :, :],
                                         QP3[64 * par:64 * par + 64, term, :]).then_inc(s_qps, 16)
            sp.wait_ge(s_pb, 6 * STEPS)
            sp.dma_start(BS, bs_d).then_inc(s_bs, 16)
            sp.wait_ge(s_pr, NB)
            sp.dma_start(W2, w2_in).then_inc(s_w2, 16)
            slots(1)
            for b in range(NB):
                sp.wait_ge(s_xr, NT + NB + TB * (b + 1))
                sp.dma_start(out[b * SEQ:(b + 1) * SEQ, :].rearrange("(n p) d -> p n d", p=P),
                             X[:, b * TB:(b + 1) * TB, :]).then_inc(s_out, 16)
            sp.wait_ge(s_out, 16 * NB)

        @block.gpsimd
        def _(pool):
            def token_numbers():
                pool.memset(Z[:, 0:P], 0.0).then_inc(s_z, 1)
                pool.memset(Z[:, P:ROW], float(2 * (NT + NS) * P)).then_inc(s_z, 1)
                pool.iota(XN1_ROWS[:, :, P], [[P, NT]], base=0, channel_multiplier=1,
                          allow_small_or_imprecise_dtypes=True).then_inc(s_z, 1)

            token_numbers()
            pool.memset(ident[:, :], 0.0).then_inc(s_c0, 1)
            pool.memset(tri[:, :], 1.0).then_inc(s_c0, 1)
            pool.memset(ones[:, :], 1.0).then_inc(s_c0, 1)
            pool.memset(utri[:, :], 1.0).then_inc(s_c0, 1)
            pool.memset(onesb[:, :], 1.0).then_inc(s_c0, 1)
            pool.memset(MA[:, :], CLIP).then_inc(s_c0, 1)
            pool.memset(MB[:, :], -1).then_inc(s_c0, 1)
            pool.memset(VF[:, :], 1.0).then_inc(s_c0, 1)
            ok = dict(allow_small_or_imprecise_dtypes=True)
            pool.iota(em8[:, :], [[1, E]], base=-E, channel_multiplier=0, **ok).then_inc(s_c0, 1)
            pool.iota(erow[:, :], [[E_ROWS, E]], base=0, channel_multiplier=0, **ok).then_inc(s_c0, 1)
            pool.iota(j128[:, :], [[P, NT]], base=0, channel_multiplier=0, **ok).then_inc(s_c0, 1)
            pool.iota(lower8[:, :, :], [[1, E], [-1, E]], base=0, channel_multiplier=0, **ok)\
                .then_inc(s_c0, 1)
            pool.iota(slot_no[:, :], [[1, NS]], base=0, channel_multiplier=0, **ok).then_inc(s_c0, 1)
            pool.iota(spare[:, :], [[P, NS]], base=NT * P, channel_multiplier=1, **ok)\
                .then_inc(s_c0, 1)
            pool.iota(seen[:, :], [[P, TB]], base=1, channel_multiplier=1, **ok).then_inc(s_c0, 1)
            pool.wait_ge(s_c0, 15)
            pool.affine_select(out=ident[:, :], in_=ident[:, :], compare_op=ALU.not_equal, fill=1.0,
                               base=0, pattern=[[-1, P]], channel_multiplier=1).then_inc(s_c, 1)
            pool.affine_select(out=tri[:, :], in_=tri[:, :], compare_op=ALU.is_ge, fill=0.0,
                               base=0, pattern=[[1, P]], channel_multiplier=-1).then_inc(s_c, 1)
            pool.affine_select(out=utri[:, :], in_=utri[:, :], compare_op=ALU.is_gt, fill=0.0,
                               base=0, pattern=[[1, P]], channel_multiplier=-1).then_inc(s_c, 1)
            pool.affine_select(out=MA[:, SEQ - P:SEQ], in_=MA[:, SEQ - P:SEQ], compare_op=ALU.is_ge,
                               fill=MASKED, base=0, pattern=[[-1, P]], channel_multiplier=1)\
                .then_inc(s_c, 1)
            for at in (0, P):
                pool.affine_select(out=MB[:, at:at + P], in_=MB[:, at:at + P], compare_op=ALU.is_ge,
                                   fill=0, base=0, pattern=[[1, P]], channel_multiplier=-1)\
                    .then_inc(s_c, 1)
            pool.tensor_scalar(lower8[:, :, :], lower8[:, :, :], 0.0, None, ALU.is_gt).then_inc(s_c, 1)

            def scatter(r):
                pool.wait_ge(s_z, 3 * (r + 1))
                for i, (n0, n1) in enumerate(ROUTE_TILES[r]):
                    pool.wait_ge(s_row, part_no(r, i))
                    for n in range(n0, n1):
                        pool.indirect_dma_start(xs_d, bass.IndirectOffsetOnAxis(posx[:, n:n + 1], 0),
                                                XN1_ROWS[:, n, :], None).then_inc(s_sct, 16)
                pool.wait_ge(s_pos, r + 1)
                load_x(pool, r, range(len(SP_SLOTS + ACT_SLOTS), NS))

            def scatter_back(r):
                for s in range(NS):
                    if s % 4 == 0:
                        pool.wait_ge(s_dest, r * GROUPS + s // 4 + 1)
                    pool.wait_ge(s_y, r * NS + s + 1)
                    pool.indirect_dma_start(y_d, bass.IndirectOffsetOnAxis(dest[:, s:s + 1], 0),
                                            YO[:, s, :], None).then_inc(s_yd, 16)

            scatter(0)
            scatter_back(0)
            for u in range(len(UNITS)):
                for c in range(2):
                    m = 2 * u + c
                    pool.wait_ge(s_mid, m + 1)
                    pool.tensor_tensor(SP3[u][:, 2, c * SEQ:(c + 1) * SEQ], REM[:, c, :],
                                       SP3[u][:, 1, c * SEQ:(c + 1) * SEQ], ALU.subtract)\
                        .then_inc(s_lo, 1)

            done = [0]

            def link(ins):
                done[0] += 1
                ins.then_inc(s_pool, 1)
                pool.wait_ge(s_pool, done[0])

            def agg_sums(b):
                pool.wait_ge(s_e, 2 * TB * HP * (b + 1))
                a = agg[:, :, :, b * HP:(b + 1) * HP].rearrange("p i par s -> p (i par) s")
                by_pair = [rt[:, k, :].rearrange("p (i s) -> p i s", s=HP) for k in range(2)]
                link(pool.tensor_scalar(by_pair[0], a, 2.0, 5 * EPS, ALU.mult, ALU.add))
                pool.tensor_scalar(by_pair[1], a, 3 * EPS, None, ALU.add).then_inc(s_apre, 1)

            def scale_q(b):
                t4 = rt[:, 1, :]
                pool.wait_ge(s_arec, b + 1)
                link(pool.tensor_scalar(t4, t4, SCALE, None, ALU.mult))
                for i in range(TB):
                    q = QT[:, b * TB + i, :].rearrange("p (par d pair) -> p par d pair", par=2, d=HD)
                    r = spread(t4[:, i * H:(i + 1) * H].rearrange(
                        "p (par o pair) -> p par o pair", par=2, o=1), 2, HD)
                    pool.tensor_tensor(q, q, r, ALU.mult).then_inc(s_qsc, 1)

            def query_part(b):
                t0, t4, s_, u_, p_, den = (rt[:, j, :] for j in range(6))
                link(pool.tensor_scalar(s_, t0, EPS, None, ALU.mult))
                link(pool.tensor_tensor(u_, s_, s_, ALU.mult))
                link(pool.tensor_scalar(p_, u_, 1.0 / 9.0, 1.0 / 7.0, ALU.mult, ALU.add))
                for c in (1.0 / 5.0, 1.0 / 3.0, 1.0):
                    link(pool.tensor_tensor(p_, p_, u_, ALU.mult))
                    link(pool.tensor_scalar(p_, p_, c, None, ALU.add))
                link(pool.tensor_tensor(p_, p_, s_, ALU.mult))
                pool.tensor_scalar(ckf(b), p_, 2.0, None, ALU.mult).then_inc(s_ck, 1)

            def key_counts(b):
                pool.wait_ge(s_ck, b + 1)
                if b:
                    pool.wait_ge(s_num, b)
                den = rt[:, 5, :]
                seen_h = spread(seen[:, :].rearrange("p (n o) -> p n o", o=1), 2, H)
                link(pool.tensor_tensor(den.rearrange("p (i h) -> p i h", i=TB), ck[:, b % 2, :, :],
                                        seen_h, ALU.mult))
                pool.tensor_scalar(den, den, EPS, None, ALU.add).then_inc(s_dpre, 1)

            def scaled_q_terms(b):
                pool.wait_ge(s_qrem, b + 1)
                if b:
                    pool.wait_ge(s_qps, STACK_DMAS * b)
                pool.tensor_copy(QP3[:, 1, :], QREM).then_inc(s_qmid, 1)
                pool.wait_ge(s_qmid, b + 1)
                pool.tensor_tensor(QP3[:, 2, :], QREM, QP3[:, 1, :], ALU.subtract).then_inc(s_qlo, 1)

            def normalise(b):
                aof = AO.rearrange("p i h c -> p (i h) c")
                numf = NUM.rearrange("p i h c -> p (i h) c")
                pool.wait_ge(s_vp, b + 1)
                pool.wait_ge(s_ao, HP * (b + 1))
                link(pool.tensor_tensor(numf, numf, aof[:, :, 0:HD], ALU.add))
                pool.wait_ge(s_drec, b + 1)
                pool.tensor_tensor(numf, numf, spread(rt[:, 5, :].rearrange("p (n o) -> p n o", o=1),
                                                      2, HD), ALU.mult).then_inc(s_num, 1)

            for s in range(END_STEP):
                for b in range(NB):
                    at = s - b * HP
                    if at == A_AT:
                        agg_sums(b)
                    if at == R_AT:
                        scale_q(b)
                    if at == Q_AT:
                        scaled_q_terms(b)
                        query_part(b)
                    if at == V_AT:
                        key_counts(b)
                    if at == N_AT + late(b):
                        normalise(b)
            pool.wait_ge(s_pa, TB * STEPS)
            token_numbers()
            scatter(1)
            scatter_back(1)

        @block.scalar
        def _(act):
            def tables(number):
                act.add_instruction(mybir.InstLoadActFuncSet(
                    name=nc.get_next_instruction_name(), act_func_set_id=number,
                    engine=mybir.EngineType.Activation, ins=[], outs=[]))

            def deviations(part):
                _, b0, b1 = LN_PARTS[part]
                act.wait_ge(s_var, part + 1)
                act.activation(lnt[:, 1, b0 * TB:b1 * TB], lnt[:, 0, b0 * TB:b1 * TB], ACT.Sqrt)\
                    .then_inc(s_std, 1)

            def copy_xnt(k, b0, b1, xnt):
                for g in range(b0, b1):
                    act.wait_ge(s_tp, NB * k + g + 1)
                    act.activation(xnt[:, g * SEQ:(g + 1) * SEQ], PS[:, g % 2, :], ACT.Copy)\
                        .then_inc(s_xnt, 1)

            def gelu(r, s, k):
                act.wait_ge(s_up, s + (r * NS + 1))
                for c in range(FC):
                    if c == 0 and (not isinstance(s, int) or s >= 2):
                        act.wait_ge(s_dn, s + (r * NS - 1))
                    last = act.activation(HT[:, k % 2, c * P:(c + 1) * P],
                                          PS[:, k % 2, c * P:(c + 1) * P], ACT.Gelu,
                                          bias=W1[:, k, F + c:F + c + 1])
                last.then_inc(s_h, 1)

            def ffn(r):
                act.wait_ge(s_sh, part_no(r, len(ROUTE_TILES[r]) - 1))
                act.activation(ex, sh, ACT.Exp).then_inc(s_ex, 1)
                pad(act, r, range(E // 2, E))
                act.wait_ge(s_pos, r + 1)
                if r:
                    act.wait_ge(s_pr, NB)
                for k in range(RING):
                    e = act.value_load(emap[0:1, k:k + 1], min_val=0, max_val=E - 1)
                    act.dma_start(W1[:, k, :], w1_in[ds(e, 1), :, :].rearrange("o p n -> p (o n)"))\
                        .then_inc(s_w1[k], 16)
                load_x(act, r, ACT_SLOTS)
                for k in range(RING):
                    gelu(r, k, k)
                with act.Fori(1, NS // RING) as g:
                    for k in range(RING):
                        gelu(r, g * RING + k, k)
                for s in range(NS // RING * RING, NS):
                    gelu(r, s, s % RING)

            deviations(0)
            copy_xnt(0, 0, 1, XNT1)
            deviations(1)
            copy_xnt(0, 1, 4, XNT1)
            ffn(0)

            def first_term(m):
                u, c = m // 2, m % 2
                act.wait_ge(s_pj, m + 1)
                if u == 5:
                    act.wait_ge(s_stk[0], STACK_DMAS)
                act.activation(SP3[u][:, 0, c * SEQ:(c + 1) * SEQ], PS[:, PJ_BANK[m // 6] + c, :],
                               ACT.Copy)\
                    .then_inc(s_hi, 1)

            def second_term(m):
                u, c = m // 2, m % 2
                act.wait_ge(s_rem, m + 1)
                act.activation(SP3[u][:, 1, c * SEQ:(c + 1) * SEQ], REM[:, c, :], ACT.Copy)\
                    .then_inc(s_mid, 1)

            def q_rows(t):
                act.wait_ge(s_qv, t + 1)
                act.activation(QT[:, 2 * t:2 * t + 2, :],
                               PS[:, QV_BANK[t // 4] + t % 2, :]
                               .rearrange("p (n c) -> p n c", n=2)[:, :, 0:P],
                               ACT.Copy).then_inc(s_qc, 1)

            deviations(2)
            copy_xnt(1, 0, 2, XNT2)
            for m in range(7):
                if m < 6:
                    first_term(m)
                if m:
                    second_term(m - 1)
            for t in range(4):
                q_rows(t)
            deviations(3)
            copy_xnt(1, 2, 4, XNT2)

            def after(s):
                if s < 6:
                    first_term(6 + s)
                if 1 <= s < 7:
                    second_term(5 + s)
                if s < 4:
                    q_rows(4 + s)
                for b in range(NB):
                    if s == b * HP + T_AT + late(b):
                        act.wait_ge(s_ot, b + 1)
                        act.wait_ge(s_qlo, min(b + 2, NB))
                        act.activation(OT, PS[:, 7, :], ACT.Copy).then_inc(s_otc, 1)

            def first_pass(s, tiles):
                for i in tiles:
                    n = (i + 1) * P
                    act.wait_ge(s_cl, 4 * s + (i + 1))
                    for par in range(2):
                        act.activation(CL[i][:, par, 0:n], CL[i][:, par, 0:n], ACT.Exp,
                                       scale=SCALE,
                                       accum_out=aggf[:, ds(s + (2 * i + par) * STEPS, 1)])\
                            .then_inc(s_e, 1)

            def second_pass(v):
                act.wait_ge(s_abs, 6 * v + 6)
                wb = weights(v)
                for w in ([wb] if wb is not None else [head_weights(v, par) for par in range(2)]):
                    last = act.activation(w, w, ACT.Ln, bias=1.0, scale=1.0)
                last.then_inc(s_ln, 1)

            def av_out(v):
                act.wait_ge(s_av, TB * (v // 2 + 1))
                if v:
                    act.wait_ge(s_aotp, v // 2)
                act.activation(AOT, PS[:, av_bank(v), :], ACT.Copy).then_inc(s_aot, 1)

            tables(EXP_AND_LN)
            for s in range(END_STEP):
                v = s - LAG
                if v < TAIL + 4 and leaving(v) is not None:
                    av_out(leaving(v))
                if s < STEPS:
                    first_pass(s, range(TB))
                if v >= TAIL + 3 and leaving(v + 1) is not None:
                    av_out(leaving(v + 1))
                if 0 <= v < STEPS:
                    second_pass(v)
                if s == TURN_EARLY:
                    copy_xnt(2, 0, 3, XNT1)
                after(s)
                if s == LN_EARLY:
                    deviations(4)
            deviations(5)
            copy_xnt(2, 3, 4, XNT1)
            ffn(1)

        @block.vector
        def _(dve):
            done = [0]

            def mark(ins, times=1):
                done[0] += times
                ins.then_inc(s_dve, 1)

            def settle():
                dve.wait_ge(s_dve, done[0])

            def link(ins):
                mark(ins)
                settle()

            def moments(b):
                for n in range(b * TB, (b + 1) * TB):
                    mark(dve.bn_stats(stats[:, n, :], X[:, n, :]))
                settle()
                for n in range(b * TB, (b + 1) * TB):
                    mark(dve.bn_aggr(mv[:, n, :], stats[:, n, :]))

            def layer_norm(part, xn):
                _, b0, b1 = LN_PARTS[part]
                var, std, inv, tmp = (lnt[:, j, b0 * TB:b1 * TB] for j in range(4))
                settle()
                dve.tensor_scalar(var, mv[:, b0 * TB:b1 * TB, 1], LN_EPS, None, ALU.add)\
                    .then_inc(s_var, 1)
                dve.wait_ge(s_std, part + 1)
                link(dve.reciprocal(inv, std))
                link(dve.tensor_tensor(tmp, inv, inv, ALU.mult))
                link(dve.tensor_tensor(tmp, tmp, var, ALU.mult))
                link(dve.tensor_scalar(tmp, tmp, -0.5, 1.5, ALU.mult, ALU.add))
                link(dve.tensor_tensor(inv, inv, tmp, ALU.mult))
                for n in range(b0 * TB, b1 * TB):
                    dve.tensor_scalar(xn[:, n, :], X[:, n, :], mv[:, n, 0:1], lnt[:, 2, n:n + 1],
                                      ALU.subtract, ALU.mult).then_inc(s_xn, 1)

            def over_n(a, k=NT):
                return spread(a.rearrange("p (o e) -> p o e", o=1), 1, k)

            def over_e(a, k=E):
                return spread(a.rearrange("p (n o) -> p n o", o=1), 2, k)

            def route(r, i):
                n0, n1 = ROUTE_TILES[r][i]
                n, part = n1 - n0, part_no(r, i)
                oh_, sh_, cand_, posm_ = (a[:, n0:n1, :] for a in (oh, sh, cand, posm))
                mx_, cmin_, posf_ = (a[:, n0:n1] for a in (mx, cmin, posf))

                def of_part(bank):
                    return PS[:, bank, n0 * E:n1 * E].rearrange("p (n e) -> p n e", n=n)

                if i == 0:
                    link(dve.memset(oh[:, NT, :], 0.0))
                dve.wait_ge(s_sc, part)
                link(dve.reduce_max(mx_, of_part(SCORE_BANKS[i]), axis=AX))
                dve.tensor_tensor(sh_, of_part(SCORE_BANKS[i]), over_e(mx_), ALU.subtract).then_inc(s_sh, 1)
                dve.wait_ge(s_sh, part)
                dve.wait_ge(s_c, 7)
                link(dve.scalar_tensor_tensor(out=cand_, in0=sh_, scalar=0.0, in1=over_n(em8[:, :], n),
                                              op0=ALU.is_ge, op1=ALU.mult))
                link(dve.tensor_reduce(cmin_, cand_, axis=AX, op=ALU.min))
                dve.tensor_tensor(oh_, over_n(em8[:, :], n), over_e(cmin_), ALU.is_equal)\
                    .then_inc(s_oh, 1)
                dve.wait_ge(s_rk, part)
                link(dve.tensor_tensor(posm_, of_part(RANK_BANKS[i]), over_n(erow[:, :], n), ALU.add))
                link(dve.tensor_tensor(posm_, posm_, oh_, ALU.mult))
                link(dve.reduce_sum(posf_, posm_, axis=AX))
                dve.tensor_copy(posx[:, n0:n1], posf_).then_inc(s_row, 1)

            def slot_map(r):
                link(dve.tensor_copy(cnt, PS[:, RANK_BANKS[len(ROUTE_TILES[r]) - 1], NT * E:NT * E + E]))
                dve.tensor_tensor(zrow, cnt, erow[:, :], ALU.add).then_inc(s_cnt, 1)
                link(dve.tensor_tensor(ntc, over_e(cnt, NT), over_n(j128[:, :], E), ALU.is_gt))
                link(dve.reduce_sum(nt, ntc, axis=AX))
                link(dve.tensor_tensor(bsm, over_n(nt, E), lower8[:, :, :], ALU.mult))
                link(dve.reduce_sum(bst, bsm, axis=AX))
                link(dve.tensor_tensor(bend, bst, nt, ALU.add))
                link(dve.tensor_tensor(mapm, over_e(slot_no[:, :]), over_n(bend, NS), ALU.is_ge))
                link(dve.reduce_sum(mapf, mapm, axis=AX))
                link(dve.tensor_scalar(mapf, mapf, float(E - 1), None, ALU.min))
                link(dve.tensor_tensor(ends, cnt, erow[:, :], ALU.add))
                link(dve.tensor_scalar(hole, nt, float(-P), float(E_ROWS), ALU.mult, ALU.add))
                link(dve.tensor_tensor(holem, mapm, over_n(hole, NS), ALU.mult))
                link(dve.reduce_sum(holes, holem, axis=AX))
                link(dve.scalar_tensor_tensor(out=rowf, in0=slot_no[:, :], scalar=float(P), in1=holes,
                                              op0=ALU.mult, op1=ALU.add))
                link(dve.tensor_scalar(used, mapm[:, :, E - 1], -1.0, 1.0, ALU.mult, ALU.add))
                link(dve.scalar_tensor_tensor(out=rowf, in0=rowf, scalar=ends[:, E - 1:E], in1=used,
                                              op0=ALU.subtract, op1=ALU.mult))
                link(dve.tensor_scalar(rowf, rowf, ends[:, E - 1:E], None, ALU.add))
                link(dve.tensor_copy(srow, rowf))
                dve.tensor_copy(emap[:, :], mapf).then_inc(s_pos, 1)
                dve.wait_ge(s_ex, r + 1)
                link(dve.reduce_sum(ssum, ex, axis=AX))
                link(dve.reciprocal(ssum, ssum))
                link(dve.tensor_scalar(coef[:, :], ssum, 0.5, None, ALU.mult))

            def copy_xt(r, g, slots):
                w = slots * P
                dve.wait_ge(s_px, g + (r * GROUPS + 1))
                dve.tensor_copy(XT[:, ds(g & 1, 1), 0:w], PS[:, ds((g & 1) + 4, 1), 0:w])\
                    .then_inc(s_vx, 1)
                dve.tensor_tensor(dest[:, ds(g * 4, slots)], XS_ROWS[:, ds(g * 4, slots), P],
                                  spare[:, ds(g * 4, slots)], ALU.min).then_inc(s_dest, 1)

            def slot_out(r, s):
                dve.wait_ge(s_dn, s + (r * NS + 1))
                dve.tensor_copy(YO[:, ds(s, 1), :], PS[:, ds((s & 1) + 6, 1), 0:P]).then_inc(s_y, 1)

            def constants():
                dve.wait_ge(s_b, 16)
                link(dve.tensor_copy(BT[:, 0, :], BL))
                link(dve.tensor_tensor(BR, BL, BT[:, 0, :], ALU.subtract))
                link(dve.tensor_copy(BT[:, 1, :], BR))
                link(dve.tensor_tensor(BR, BR, BT[:, 1, :], ALU.subtract))
                dve.tensor_copy(BT[:, 2, :], BR).then_inc(s_bt, 1)
                dve.wait_ge(s_c, 7)
                link(dve.tensor_scalar(MB[:, :], MB[:, :], 1, None, ALU.logical_shift_right))

            def ffn(r):
                route(r, len(ROUTE_TILES[r]) - 1)
                slot_map(r)
                if r == 0:
                    constants()

                copy_xt(r, 0, 4)
                with dve.Fori(0, GROUPS - 2) as g:
                    copy_xt(r, g + 1, 4)
                    for k in range(4):
                        slot_out(r, g * 4 + k)
                copy_xt(r, GROUPS - 1, NS - 4 * (GROUPS - 1))
                for s in range(4 * (GROUPS - 2), NS):
                    slot_out(r, s)

            def residual(r, b):
                dve.wait_ge(s_yg[b], 16 * (r + 1))
                for n in range(b * TB, (b + 1) * TB):
                    dve.scalar_tensor_tensor(out=X[:, n, :], in0=YG[:, n, :],
                                             scalar=coef[:, n:n + 1], in1=X[:, n, :],
                                             op0=ALU.mult, op1=ALU.add).then_inc(s_xr, 1)
                if r == 0:
                    dve.wait_ge(s_xr, TB * (b + 1))
                    moments(b)

            for part in range(2):
                for b in (2 * part, 2 * part + 1):
                    dve.wait_ge(s_x[b], 16)
                    moments(b)
                layer_norm(part, XN1)
            route(0, 0)
            ffn(0)

            def remainder(m):
                u, c = m // 2, m % 2
                dve.wait_ge(s_hi, m + 1)
                if m >= 2:
                    dve.wait_ge(s_lo, m - 1)
                dve.tensor_tensor(REM[:, c, :], PS[:, PJ_BANK[m // 6] + c, :], SP3[u][:, 0, c * SEQ:(c + 1) * SEQ],
                                  ALU.subtract).then_inc(s_rem, 1)

            def v_rows(t):
                dve.wait_ge(s_qc, t + 1)
                for k in range(2):
                    dve.tensor_copy(V[:, 2 * t + k, :, 0:HD],
                                    PS[:, QV_BANK[t // 4] + t % 2, k * 2 * P + P:(k + 1) * 2 * P].rearrange(
                                        "p (h c) -> p h c", h=H)).then_inc(s_vc, 1)

            residual(0, 0)
            residual(0, 1)
            layer_norm(2, XN2)
            residual(0, 2)
            remainder(0)
            remainder(1)
            residual(0, 3)
            for m in range(2, 6):
                remainder(m)
            for t in range(4):
                v_rows(t)
            layer_norm(3, XN2)

            def clip_scores(s, i, first):
                n = (i + 1) * P
                dve.wait_ge(s_pa, 4 * s + (i + 1))
                if not first:
                    dve.wait_ge(s_e, 8 * s + (2 * i - 6))
                bank = 2 * (i % 2)
                dve.scalar_tensor_tensor(
                    out=CL[i][:, :, 0:n], in0=PS[:, bank:bank + 2, 0:n], scalar=-CLIP,
                    in1=spread(MA[:, SEQ - n:SEQ].rearrange("p (o n) -> p o n", o=1), 1, 2),
                    op0=ALU.max, op1=ALU.min).then_inc(s_cl, 1)

            def abs_scores(v, k, alone):
                par, g = k % 2, k // 2
                n, at = SEG_N[g], 512 * g
                dve.wait_ge(s_pb, 6 * v + (k + 1))
                last = v - 4 if v >= TAIL + 3 else v - 3
                if v == 2 and k == 0:
                    dve.wait_ge(s_stk[2], STACK_DMAS)
                    dve.wait_ge(s_stk[5], STACK_DMAS)
                elif v == TAIL + 3 and k == 0:
                    dve.wait_ge(s_e, 2 * TB * STEPS)
                    dve.wait_ge(s_qt, NB)
                elif v >= 3 and v != TAIL + 3 and par == 0:
                    dve.wait_ge(s_av, TB * (last // 2) + (1, 3, 4)[g])
                bank = b_bank(k, alone)
                dve.tensor_tensor(
                    head_weights(v, par)[:, at:at + n].bitcast(i32), PS[:, bank, 0:n].bitcast(i32),
                    MB[:, SEG_MASK[g]:SEG_MASK[g] + n], ALU.bitwise_and).then_inc(s_abs, 1)

            def heads_out(v, tail):
                dve.wait_ge(s_aotp, v // 2 + 1)
                w = 2 * (HD + 1)
                for par in range(2):
                    at = v % HP * (HD + 1) + par * HP * (HD + 1)
                    dve.tensor_copy(
                        AO.rearrange("p i h c -> p i (h c)")[:, :, at:at + w],
                        PS[:, b_bank(AO_K, tail), AO_COL:AO_COL + TB * 2 * w].rearrange("p (i r) -> p i r", i=TB)
                        [:, :, par * w:(par + 1) * w]).then_inc(s_ao, 1)

            def v_prefix(b):
                dve.wait_ge(s_cv, b + 1)
                dve.wait_ge(s_ck, b + 1)
                if b:
                    dve.wait_ge(s_ot, b)
                dve.tensor_tensor(NUM.rearrange("p i h c -> p (i h) c"),
                                  PS[:, 7, :].rearrange("p (h c) -> p h c", c=HD),
                                  over_e(ckf(b), HD), ALU.mult).then_inc(s_vp, 1)

            def scaled_q_terms(b):
                dve.wait_ge(s_qt, b + 1)
                if b:
                    dve.wait_ge(s_qps, STACK_DMAS * b)
                dve.tensor_copy(QP3[:, 0, :], PS[:, 7, :]).then_inc(s_qhi, 1)
                dve.wait_ge(s_qhi, b + 1)
                dve.tensor_tensor(QREM, PS[:, 7, :], QP3[:, 0, :], ALU.subtract).then_inc(s_qrem, 1)

            def after(s):
                if 1 <= s < 7:
                    remainder(5 + s)
                if 1 <= s < 5:
                    v_rows(3 + s)
                for b in range(NB):
                    at = s - b * HP
                    if at == R_AT:
                        dve.wait_ge(s_apre, b + 1)
                        dve.reciprocal(rt[:, 0:2, :], rt[:, 0:2, :]).then_inc(s_arec, 1)
                    if at == Q_AT:
                        scaled_q_terms(b)
                    if at == V_AT:
                        v_prefix(b)
                    if at == N_AT + late(b):
                        dve.wait_ge(s_dpre, b + 1)
                        dve.wait_ge(s_ao, HP * (b + 1))
                        den = rt[:, 5, :]
                        link(dve.tensor_tensor(den, den, AO.rearrange("p i h c -> p (i h) c")[:, :, HD],
                                               ALU.add))
                        dve.reciprocal(den, den).then_inc(s_drec, 1)
                    if at == X_AT + late(b):
                        dve.wait_ge(s_pr, b + 1)
                        xb = X[:, b * TB:(b + 1) * TB, :]
                        dve.tensor_tensor(xb, PS[:, 7, :].rearrange("p (n d) -> p n d", n=TB), xb,
                                          ALU.add).then_inc(s_xr, 1)
                        dve.wait_ge(s_xr, NT + b + 1)
                        moments(b)

            dve.wait_ge(s_stk[1], STACK_DMAS)
            for s in range(END_STEP):
                v = s - LAG
                if v == 0:
                    dve.wait_ge(s_lo, 12)
                for k in range(6):
                    if s < STEPS and k < TB:
                        clip_scores(s, k, s == 0)
                    if 0 <= v < STEPS:
                        abs_scores(v, k, s >= STEPS)
                    if k == AO_K and leaving(v) is not None:
                        heads_out(leaving(v), s >= STEPS)
                if s == TURN_EARLY + 2:
                    route(1, 0)
                after(s)
                if s == LN_EARLY:
                    layer_norm(4, XN1)
            layer_norm(5, XN1)
            route(1, 1)
            ffn(1)
            for b in range(NB):
                residual(1, b)

        @block.tensor
        def _(pe):
            def layer_norm(part, xn):
                k, b0, b1 = LN_PARTS[part]
                for g in range(b0, b1):
                    pe.wait_ge(s_xn, NT * k + TB * (g + 1))
                    if g >= 2:
                        pe.wait_ge(s_xnt, NB * k + g - 1)
                    for j in range(TB):
                        last = pe.transpose(PS[:, g % 2, j * P:(j + 1) * P], xn[:, g * TB + j, :],
                                            ident[:, :])
                    last.then_inc(s_tp, 1)

            def gate(r, i, n0, n1):
                for n in range(n0, n1):
                    if n % TB == 0:
                        pe.wait_ge(s_xnt, 2 * NB * r + n // TB + 1)
                    last = pe.matmul(PS[:, SCORE_BANKS[i], n * E:(n + 1) * E], XNT1[:, n * P:(n + 1) * P],
                                     WG[:, :], start=True, stop=True)
                if n1 == ROUTE_TILES[r][i][1]:
                    last.then_inc(s_sc, 1)

            def ranks(r, i):
                n0, n1 = ROUTE_TILES[r][i]
                end = n1 + (n1 == NT)
                pe.wait_ge(s_oh, part_no(r, i))
                pe.matmul(PS[:, RANK_BANKS[i], n0 * E:end * E], utri[:, :], oh[:, n0:end, :],
                          start=True, stop=False)
                for n in range(end - 1):
                    first = max(n + 1, n0)
                    last = pe.matmul(PS[:, RANK_BANKS[i], first * E:end * E], onesb[:, :],
                                     spread(oh[:, n:n + 1, :], 1, end - first), start=False,
                                     stop=n == end - 2)
                last.then_inc(s_rk, 1)

            def slot_transposes(r, g):
                pe.wait_ge(s_xs[r][g], 16 * min(4, NS - 4 * g))
                if g >= 2:
                    pe.wait_ge(s_vx, r * GROUPS + g - 1)
                for s in range(4 * g, min(4 * g + 4, NS)):
                    last = pe.transpose(PS[:, 4 + g % 2, (s % 4) * P:(s % 4 + 1) * P], XS[:, s, :],
                                        ident[:, :])
                last.then_inc(s_px, 1)

            def up(r, s):
                if s % 4 == 0:
                    pe.wait_ge(s_vx, r * GROUPS + s // 4 + 1)
                if s >= 2:
                    pe.wait_ge(s_h, r * NS + s - 1)
                pe.wait_ge(s_w1[s % RING], 16 * (r * ring_uses(s % RING) + s // RING + 1))
                for c in range(FC):
                    last = pe.matmul(PS[:, s % 2, c * P:(c + 1) * P],
                                     W1[:, s % RING, c * P:(c + 1) * P],
                                     XT[:, s // 4 % 2, (s % 4) * P:(s % 4 + 1) * P],
                                     start=True, stop=True)
                last.then_inc(s_up, 1)

            def down(r, s):
                e = pe.value_load(emap[0:1, s:s + 1], min_val=0, max_val=E - 1)
                if s == 0:
                    pe.wait_ge(s_bs, 16 * (r + 1))
                pe.wait_ge(s_h, r * NS + s + 1)
                if s >= 2:
                    pe.wait_ge(s_y, r * NS + s - 1)
                pe.matmul(PS[:, 6 + s % 2, 0:P], onesb[0:TERMS, :], BS[:, ds(e * P, P)],
                          start=True, stop=False)
                for c in range(FC):
                    last = pe.matmul(PS[:, 6 + s % 2, 0:P], HT[:, s % 2, c * P:(c + 1) * P],
                                     W2[:, ds(e * F + c * P, P)], start=False, stop=c == FC - 1)
                last.then_inc(s_dn, 1)

            def ring_uses(k):
                return len(range(k, NS, RING))

            def ffn(r):
                gate(r, len(ROUTE_TILES[r]) - 1, *ROUTE_TILES[r][-1])
                ranks(r, len(ROUTE_TILES[r]) - 1)
                pe.wait_ge(s_pos, r + 1)
                slot_transposes(r, 0)
                for s in range(NS + 1):
                    if s < NS:
                        up(r, s)
                        if s % 4 == 1 and s // 4 + 1 < GROUPS:
                            slot_transposes(r, s // 4 + 1)
                    if s == 1:
                        pe.wait_ge(s_w2, 16 * (r + 1))
                    if s >= 1:
                        down(r, s - 1)

            pe.wait_ge(s_c, 7)
            pe.wait_ge(s_wg, 16)
            layer_norm(0, XN1)
            gate(0, 0, *ROUTE_TILES[0][0])
            layer_norm(1, XN1)
            ranks(0, 0)
            ffn(0)

            def project(m):
                which, w = UNITS[m // 2]
                if m >= 2:
                    pe.wait_ge(s_hi, m - 1)
                    pe.wait_ge(s_rem, m - 1)
                at = w * 2 * SEQ + (m % 2) * SEQ
                pe.matmul(PS[:, PJ_BANK[m // 6] + m % 2, :], WA[:, WCOL[which], :], XNT2[:, at:at + SEQ],
                          start=True, stop=True).then_inc(s_pj, 1)

            def q_v_rows(t):
                if t >= 2:
                    pe.wait_ge(s_qc, t - 1)
                    pe.wait_ge(s_vc, 2 * (t - 1))
                for k in range(2):
                    n = 2 * t + k
                    last = pe.matmul(PS[:, QV_BANK[t // 4] + t % 2, k * 2 * P:(k + 1) * 2 * P],
                                     XNT2[:, n * P:(n + 1) * P], WA[:, 0:2, :], start=True, stop=True)
                last.then_inc(s_qv, 1)

            pe.wait_ge(s_wa, 16)
            layer_norm(2, XN2)
            pe.wait_ge(s_xnt, NB + 2)
            for m in range(6):
                project(m)
            for t in range(4):
                q_v_rows(t)
            pe.wait_ge(s_hi, 6)
            pe.wait_ge(s_rem, 6)
            layer_norm(3, XN2)
            pe.wait_ge(s_xnt, 2 * NB)

            def scores_a(s, i):
                b, hp, n = s // HP, s % HP, (i + 1) * P
                a = 4 * s + i
                if a >= 2:
                    pe.wait_ge(s_cl, a - 1)
                for par in range(2):
                    rows = slice(64 * par, 64 * par + KROWS)
                    last = pe.matmul(PS[:, 2 * (i % 2) + par, 0:n],
                                     QS[rows, hp, (b * TB + i) * P:(b * TB + i + 1) * P],
                                     YS[rows, hp, b * SEQ:b * SEQ + n], start=True, stop=True)
                last.then_inc(s_pa, 1)

            def scores_b(v, k, alone):
                b, hp, par, g = v // HP, v % HP, k % 2, k // 2
                c = 6 * v + k
                if alone:
                    if v == TAIL and k < 3:
                        pe.wait_ge(s_cl, TB * STEPS)
                    else:
                        pe.wait_ge(s_abs, c - (1 if k == 0 else 3 if k == 4 else
                                               4 if k == 3 and v == TAIL else 5))
                    if k in (0, 3) and left(v):
                        pe.wait_ge(s_ao, 2 * left(v))
                elif c >= 2:
                    pe.wait_ge(s_abs, c - 1)
                if not alone and k == 0 and v % 2 == 0 and v >= 4:
                    pe.wait_ge(s_ao, v - 2)
                rows = slice(64 * par, 64 * par + KROWS)
                at = 0
                for j in SEG_J[g]:
                    n = SEQ - j * P
                    last = pe.matmul(PS[:, b_bank(k, alone), at:at + n],
                                     KS[rows, hp, (b * TB + j) * P:(b * TB + j + 1) * P],
                                     QPS[rows, b % 2, hp, j * P:SEQ], start=True, stop=True)
                    at += n
                last.then_inc(s_pb, 1)

            def weigh(v, piece):
                j = WEIGH_TILES[piece]
                if piece == 0:
                    pe.wait_ge(s_ln, v + 2)
                    if v == TAIL:
                        pe.wait_ge(s_cl, TB * STEPS)
                    elif v >= 2:
                        pe.wait_ge(s_aot, v // 2 - (1 if v >= TAIL else 0))
                b = v // HP
                for u in (v, v + 1):
                    for par in range(2):
                        quad = QUAD * (2 * par + u % 2)
                        head = ((b * TB + j) * H + par * HP + u % HP) * (HD + 1)
                        last = pe.matmul(PS[quad:quad + QUAD, av_bank(v), j * P:SEQ],
                                         VF[:, head:head + QUAD],
                                         head_weights(u, par)[:, J_OFF[j]:J_OFF[j] + SEQ - j * P],
                                         start=piece == 0, stop=piece == TB - 1)
                last.then_inc(s_av, 1)

            def weighed_t(v, step):
                pe.wait_ge(s_aot, v // 2 + 1)
                pe.wait_ge(s_abs, min(6 * step + (1 if step >= TAIL else AO_K - 1), 6 * STEPS))
                if v >= 2:
                    pe.wait_ge(s_ao, v // 2 * 2)
                used = ident[:, :].rearrange("p (q r) -> p q r", r=QUAD)[:, :, 0:HD + 1]
                for i in range(TB):
                    at = AO_COL + i * 4 * (HD + 1)
                    last = pe.matmul(PS[:, b_bank(AO_K, step >= TAIL), at:at + 4 * (HD + 1)], AOT[:, i * P:(i + 1) * P],
                                     used, start=True, stop=True)
                last.then_inc(s_aotp, 1)

            def v_prefix(b, shift):
                if shift == 0:
                    if b + 1 < NB:
                        pe.wait_ge(s_qrem, b + 2)
                    if b:
                        pe.wait_ge(s_xr, NT + b)
                last = pe.matmul(PS[:, 7, shift * P:SEQ], (ones if shift else tri)[:, :],
                                 V[:, b * TB:(b + 1) * TB - shift, :, 0:HD], start=shift == 0,
                                 stop=shift == TB - 1)
                if shift == TB - 1:
                    last.then_inc(s_cv, 1)

            def after(s):
                if s < 6:
                    project(6 + s)
                if s < 4:
                    q_v_rows(4 + s)
                if s == 6:
                    pe.wait_ge(s_rem, 12)
                    pe.wait_ge(s_qc, NT // 2)
                    pe.wait_ge(s_vc, NT)
                for b in range(NB):
                    at = s - b * HP
                    if at == Q_AT:
                        pe.wait_ge(s_qsc, TB * (b + 1))
                        if b >= 2:
                            pe.wait_ge(s_xr, NT + b - 1)
                        for i in range(TB):
                            last = pe.transpose(PS[:, 7, i * P:(i + 1) * P], QT[:, b * TB + i, :],
                                                ident[:, :])
                        last.then_inc(s_qt, 1)
                    if at == T_AT + late(b):
                        pe.wait_ge(s_num, b + 1)
                        for i in range(TB):
                            last = pe.transpose(PS[:, 7, i * P:(i + 1) * P],
                                                NUM[:, i, :, :].rearrange("p h c -> p (h c)"), ident[:, :])
                        last.then_inc(s_ot, 1)
                    if at == P_AT + late(b):
                        pe.wait_ge(s_otc, b + 1)
                        for i in range(TB):
                            last = pe.matmul(PS[:, 7, i * P:(i + 1) * P], OT[:, i * P:(i + 1) * P],
                                             WA[:, 4, :], start=True, stop=True)
                        last.then_inc(s_pr, 1)

            pe.wait_ge(s_qc, 4)
            pe.wait_ge(s_vc, 8)
            for s in range(END_STEP):
                v = s - LAG
                for u, (which, w) in enumerate(UNITS):
                    if (v if which == 2 else s) == w * 2 * HP:
                        pe.wait_ge(s_stk[u], STACK_DMAS)
                if 0 <= v < STEPS and v % HP == 0:
                    pe.wait_ge(s_qps, STACK_DMAS * (v // HP + 1))
                for k in range(6):
                    if s < STEPS and k < TB:
                        scores_a(s, k)
                    if k == AO_K and leaving(v) is not None:
                        weighed_t(leaving(v), v)
                    if 0 <= v < STEPS:
                        scores_b(v, k, s >= STEPS)
                    if k < TB and s % HP == C_AT % HP and 0 <= s - C_AT < STEPS:
                        v_prefix((s - C_AT) // HP, k)
                    if v % 2 == 0 and 2 <= v <= TAIL:
                        for piece in PIECES.get(k, ()):
                            weigh(v - 2, piece)
                    if v % 2 == 1 and 3 <= v <= TAIL + 1:
                        for piece in PIECES.get(k + 6, ()):
                            weigh(v - 3, piece)
                    if v % 2 == 1 and TAIL + 3 <= v <= STEPS + 1:
                        for piece in TAIL_PIECES.get(k, ()):
                            weigh(v - 3, piece)
                if s == TURN_EARLY:
                    pe.wait_ge(s_abs, 6 * STEPS)
                    pe.wait_ge(s_ao, STEPS)
                    pe.wait_ge(s_aot, STEPS // 2)
                    layer_norm(4, XN1)
                after(s)
                if s == TURN_EARLY + 1:
                    gate(1, 0, *ROUTE_TILES[1][0])
                if s == TURN_EARLY + 2:
                    ranks(1, 0)
                    gate(1, 1, *ROUTE_TILES[1][1])
            layer_norm(5, XN1)
            ranks(1, 1)
            ffn(1)


def kernel(L0_attn_x, L0_attn_w_qkv, L0_attn_w_ky, L0_attn_w_proj, L0_ffn_Wg, L0_ffn_W1, L0_ffn_b1,
           L0_ffn_W2, L0_ffn_b2):
    import concourse.bacc as bacc
    from concourse.bass_utils import run_bass_kernel_spmd

    def c(a):
        return np.ascontiguousarray(a)

    wq, wk, wv = np.split(np.asarray(L0_attn_w_qkv), 3, axis=0)

    def by_channel(w):
        return np.transpose(np.asarray(w).reshape(HP, 2, HD, P), (1, 2, 0, 3)).reshape(P, P).T

    def by_head(w):
        return np.transpose(np.asarray(w).reshape(HP, 2, HD, P), (1, 0, 2, 3)).reshape(P, P).T

    proj = np.transpose(np.asarray(L0_attn_w_proj).reshape(P, HP, 2, HD), (2, 1, 3, 0)).reshape(P, P)
    wattn = np.stack([by_channel(wq), by_head(wv), by_channel(L0_attn_w_ky), by_channel(wk), proj], 1)
    arrays = {
        "x": c(np.asarray(L0_attn_x).reshape(NT * P, P)),
        "wattn": c(wattn),
        "wg": c(np.asarray(L0_ffn_Wg).T),
        "w1": c(np.concatenate([np.transpose(np.asarray(L0_ffn_W1), (0, 2, 1)),
                                np.transpose(np.asarray(L0_ffn_b1).reshape(E, FC, P), (0, 2, 1))], 2)),
        "w2": c(np.transpose(np.asarray(L0_ffn_W2).reshape(E, P, FC, P), (3, 0, 2, 1)).reshape(P, E * F)),
        "b2": c(L0_ffn_b2),
    }
    nc = bacc.Bacc("TRN2", target_bir_lowering=False, num_devices=1)
    args = [nc.dram_tensor(n, a.shape, mybir.dt.from_np(a.dtype), kind="ExternalInput").ap()
            for n, a in arrays.items()]
    out = nc.dram_tensor("out", (NT * P, P), mybir.dt.float32, kind="ExternalOutput").ap()
    build(nc, *args, out)
    r = run_bass_kernel_spmd(nc, [arrays], core_ids=[0])
    return r.results[0]["out"].reshape(NB, SEQ, P)
```
